# Optimizing a Trainium2 kernel written in Bass

```python
import numpy as np
import jax
import jax.numpy as jnp

def _softmax(x, axis=-1):
    return jax.nn.softmax(x, axis=axis)

def _gelu(x):
    return jax.nn.gelu(x, approximate=True)

def _silu(x):
    return jax.nn.silu(x)

def _sigmoid(x):
    return jax.nn.sigmoid(x)

def _layernorm(x, axis=-1, eps=1e-05):
    m = jnp.mean(x, axis=axis, keepdims=True)
    v = jnp.var(x, axis=axis, keepdims=True)
    return (x - m) / jnp.sqrt(v + eps)

def _scatter_add(tgt, idx, src, axis=0):
    return tgt.at[idx].add(src)

def _segment_sum(src, seg, n):
    return jax.ops.segment_sum(src, seg, n)
kernel_name = 'mk_flamingo_gated_d1_seqx_r8_30b392'

def setup_inputs(seed: int=0):
    np.random.seed(seed)
    _w = jnp.asarray

    def _rec_inputs():
        import jax
        import jax.numpy as jnp
        _rk = jax.random.key(seed)
        x = -0.0003929 + 0.9999 * jax.random.normal(jax.random.fold_in(_rk, 1), (32, 64, 512), jnp.float32)
        _lenS = 64 - jax.random.randint(jax.random.fold_in(_rk, 7), (32,), 0, max(1, 64 // 4) + 1, jnp.int32)
        _lenS2 = 64 - jax.random.randint(jax.random.fold_in(_rk, 8), (32,), 0, max(1, 64 // 4) + 1, jnp.int32)
        _ctx_4096P = jax.random.normal(jax.random.fold_in(_rk, 11), (32, 16, 512), jnp.float32)
        _ctx_4096c = jax.random.dirichlet(jax.random.fold_in(_rk, 511), 0.3 * jnp.ones((16,), jnp.float32), (32, 64))
        _ctx_4096t = jnp.einsum('bsk,bkd->bsd', _ctx_4096c, _ctx_4096P)
        _ctx_4096t = _ctx_4096t * jax.lax.rsqrt(jnp.mean(jnp.square(_ctx_4096t)) + 1e-12) * 0.953939
        ctx_4096 = 2.81802e-05 + 1.00001 * (_ctx_4096t + 0.3 * jax.random.normal(jax.random.fold_in(_rk, 611), (32, 64, 512), jnp.float32))
        pos_BxS2 = jnp.broadcast_to(jnp.arange(64, dtype=jnp.int32), (32, 64))
        _validS = jnp.arange(64)[None, :] < _lenS[:, None]
        _validS2 = jnp.arange(64)[None, :] < _lenS2[:, None]
        _causal = jnp.tril(jnp.ones((64, 64), dtype=bool))
        mask_BxSxS2_ik0 = jnp.where(jnp.broadcast_to(_validS2[:, None, :], (32, 64, 64)), 0, 1).astype(jnp.int32)
        _g = jax.random.normal(jax.random.fold_in(_rk, 9001), (2, 1), jnp.float32)
        _g = jnp.sign(_g) * jnp.maximum(jnp.abs(_g), 1.0) + (_g == 0) * 1.0
        g_xattn = _g[0]
        g_ffn = _g[1]
        return (x, ctx_4096, pos_BxS2, mask_BxSxS2_ik0, g_xattn, g_ffn)
    x, ctx_4096, pos_BxS2, mask_BxSxS2_ik0, g_xattn, g_ffn = _rec_inputs()

    def _L0_xattn_setup():
        import jax, jax.numpy as jnp
        import numpy as np
        B, S, E = (2, 256, 512)
        H, KVH, D = (32, 8, 128)
        GROUPS = H // KVH
        MAX_POS = 512
        ROPE_THETA = 10000.0

        def _rope_tables(max_pos, dim, theta):
            inv_freq = 1.0 / theta ** (jnp.arange(0, dim, 2, dtype=jnp.float32) / dim)
            t = jnp.arange(max_pos, dtype=jnp.float32)
            freqs = jnp.einsum('i,j->ij', t, inv_freq)
            emb = jnp.concatenate([freqs, freqs], axis=-1)
            return (jnp.cos(emb), jnp.sin(emb))

        def _rotate_half(x):
            x1, x2 = (x[..., :x.shape[-1] // 2], x[..., x.shape[-1] // 2:])
            return jnp.concatenate([-x2, x1], axis=-1)
        key = jax.random.key(seed)
        ks = jax.random.split(key, 8)
        scale_w = 1.0 / np.sqrt(E)
        query = jax.random.normal(ks[0], (B, S, E), dtype=jnp.float32)
        k_in = jax.random.normal(ks[1], (B, S, E), dtype=jnp.float32)
        v_in = jax.random.normal(ks[2], (B, S, E), dtype=jnp.float32)
        position_ids = jnp.broadcast_to(jnp.arange(S, dtype=jnp.int64), (B, S))
        src_mask = jnp.tril(jnp.ones((S, S), dtype=jnp.int32))
        src_mask = jnp.broadcast_to(src_mask, (B, S, S))
        Wq = jax.random.normal(ks[3], (E, H * D), dtype=jnp.float32) * scale_w
        Wk = jax.random.normal(ks[4], (E, KVH * D), dtype=jnp.float32) * scale_w
        Wv = jax.random.normal(ks[5], (E, KVH * D), dtype=jnp.float32) * scale_w
        Wo = jax.random.normal(ks[6], (H * D, E), dtype=jnp.float32) * scale_w
        return {'query': query, 'key': k_in, 'value': v_in, 'position_ids': position_ids, 'src_mask': src_mask, 'Wq': Wq, 'Wk': Wk, 'Wv': Wv, 'Wo': Wo}
    _L0_xattn_all = _L0_xattn_setup()
    _L0_xattn_in = {k: v for k, v in _L0_xattn_all.items() if k in ('Wq', 'Wk', 'Wv', 'Wo')}
    del _L0_xattn_all

    def _L0_ffn_setup():
        import jax, jax.numpy as jnp
        import numpy as np
        IN_F = 512
        OUT_F = 512
        RANK = 8
        NUM_EXPERTS = 64
        TOP_K = 16
        ROUTER_DIM = 16
        ALPHA = 32
        SCALING = ALPHA / TOP_K
        BOTTLENECK = NUM_EXPERTS * RANK
        key = jax.random.key(seed)
        ks = jax.random.split(key, 5)
        x = jax.random.normal(ks[0], (4, 512, IN_F), dtype=jnp.float32)
        bound_a = float(np.sqrt(6.0 / IN_F))
        A_w = jax.random.uniform(ks[1], (BOTTLENECK, IN_F), jnp.float32, -bound_a, bound_a)
        B_w = jax.random.normal(ks[2], (OUT_F, BOTTLENECK), dtype=jnp.float32) * 0.02
        Wq_w = jax.random.normal(ks[3], (ROUTER_DIM, IN_F), dtype=jnp.float32) * 0.02
        keys = jax.random.normal(ks[4], (NUM_EXPERTS, ROUTER_DIM), dtype=jnp.float32) * 0.01
        return {'x': x, 'A_w': A_w, 'B_w': B_w, 'Wq_w': Wq_w, 'keys': keys}
    _L0_ffn_all = _L0_ffn_setup()
    _L0_ffn_in = {k: v for k, v in _L0_ffn_all.items() if k in ('A_w', 'B_w', 'Wq_w', 'keys')}
    del _L0_ffn_all
    return {'x': x, 'ctx_4096': ctx_4096, 'pos_BxS2': pos_BxS2, 'mask_BxSxS2_ik0': mask_BxSxS2_ik0, 'g_xattn': g_xattn, 'g_ffn': g_ffn, 'L0_xattn_Wq': _L0_xattn_in['Wq'], 'L0_xattn_Wk': _L0_xattn_in['Wk'], 'L0_xattn_Wv': _L0_xattn_in['Wv'], 'L0_xattn_Wo': _L0_xattn_in['Wo'], 'L0_ffn_A_w': _L0_ffn_in['A_w'], 'L0_ffn_B_w': _L0_ffn_in['B_w'], 'L0_ffn_Wq_w': _L0_ffn_in['Wq_w'], 'L0_ffn_keys': _L0_ffn_in['keys']}

def reference(x, ctx_4096, pos_BxS2, mask_BxSxS2_ik0, g_xattn, g_ffn, L0_xattn_Wq, L0_xattn_Wk, L0_xattn_Wv, L0_xattn_Wo, L0_ffn_A_w, L0_ffn_B_w, L0_ffn_Wq_w, L0_ffn_keys):
    import jax
    import jax.numpy as jnp

    def _L0_xattn_ref(query, key, value, position_ids, src_mask, Wq, Wk, Wv, Wo):
        import jax, jax.numpy as jnp
        import numpy as np
        B, S, E = (2, 256, 512)
        H, KVH, D = (32, 8, 128)
        GROUPS = H // KVH
        MAX_POS = 512
        ROPE_THETA = 10000.0

        def _rope_tables(max_pos, dim, theta):
            inv_freq = 1.0 / theta ** (jnp.arange(0, dim, 2, dtype=jnp.float32) / dim)
            t = jnp.arange(max_pos, dtype=jnp.float32)
            freqs = jnp.einsum('i,j->ij', t, inv_freq)
            emb = jnp.concatenate([freqs, freqs], axis=-1)
            return (jnp.cos(emb), jnp.sin(emb))

        def _rotate_half(x):
            x1, x2 = (x[..., :x.shape[-1] // 2], x[..., x.shape[-1] // 2:])
            return jnp.concatenate([-x2, x1], axis=-1)
        nb, q_len, _ = query.shape
        q = (query @ Wq).reshape(nb, q_len, H, D).transpose(0, 2, 1, 3)
        k = (key @ Wk).reshape(nb, q_len, KVH, D).transpose(0, 2, 1, 3)
        v = (value @ Wv).reshape(nb, q_len, KVH, D).transpose(0, 2, 1, 3)
        cos_t, sin_t = _rope_tables(MAX_POS, D, ROPE_THETA)
        cos = cos_t[position_ids][:, None]
        sin = sin_t[position_ids][:, None]
        q = q * cos + _rotate_half(q) * sin
        k = k * cos + _rotate_half(k) * sin
        k = jnp.repeat(k, GROUPS, axis=1)
        v = jnp.repeat(v, GROUPS, axis=1)
        scores = jnp.einsum('bhqd,bhkd->bhqk', q, k) / jnp.sqrt(jnp.float32(D))
        mask = src_mask[:, None]
        scores = jnp.where(mask == 0, jnp.float32(-1000000000.0), scores)
        attn = jax.nn.softmax(scores, axis=-1)
        x = jnp.einsum('bhqk,bhkd->bhqd', attn, v)
        x = x.transpose(0, 2, 1, 3).reshape(nb, q_len, H * D)
        return x @ Wo

    def _L0_ffn_ref(x, A_w, B_w, Wq_w, keys):
        import jax, jax.numpy as jnp
        import numpy as np
        IN_F = 512
        OUT_F = 512
        RANK = 8
        NUM_EXPERTS = 64
        TOP_K = 16
        ROUTER_DIM = 16
        ALPHA = 32
        SCALING = ALPHA / TOP_K
        BOTTLENECK = NUM_EXPERTS * RANK
        q = jnp.einsum('bsd,rd->bsr', x, Wq_w)
        scores = jnp.einsum('bsr,er->bse', q, keys)
        top_vals, top_idx = jax.lax.top_k(scores, TOP_K)
        top_w = jax.nn.softmax(top_vals, axis=-1)
        gate = jnp.sum(jax.nn.one_hot(top_idx, NUM_EXPERTS, dtype=top_w.dtype) * top_w[..., None], axis=-2)
        z = jnp.einsum('bsd,nd->bsn', x, A_w)
        z = z.reshape(*z.shape[:-1], NUM_EXPERTS, RANK)
        z_gated = (z * gate[..., None]).reshape(*z.shape[:-2], BOTTLENECK)
        out = jnp.einsum('bsn,on->bso', z_gated, B_w) * SCALING
        return out
    x = x + jnp.tanh(g_xattn[0]) * _L0_xattn_ref(_layernorm(x, axis=-1), ctx_4096, ctx_4096, pos_BxS2, mask_BxSxS2_ik0, L0_xattn_Wq, L0_xattn_Wk, L0_xattn_Wv, L0_xattn_Wo)
    x = x + jnp.tanh(g_ffn[0]) * _L0_ffn_ref(_layernorm(x, axis=-1), L0_ffn_A_w, L0_ffn_B_w, L0_ffn_Wq_w, L0_ffn_keys)
    return x

_drawn_inputs = setup_inputs


def setup_inputs(seed=0):
    import zlib

    import numpy as np

    out = dict(_drawn_inputs(seed))
    spreads = {}
    factors = {'L0_ffn_A_w': 2.706, 'L0_ffn_Wq_w': 3.057, 'L0_ffn_keys': 3.163}
    for name, (base, spread) in spreads.items():
        noise = np.random.default_rng([zlib.crc32(name.encode()), seed]).standard_normal(out[name].shape)
        drawn = base * np.exp(spread * noise) if base else spread * noise
        out[name] = jnp.asarray(drawn.astype(out[name].dtype))
    for name, factor in factors.items():
        out[name] = (out[name] * factor).astype(out[name].dtype)
    return out
```

```python
from contextlib import ExitStack

import concourse.bass as bass
from concourse import mybir

F32 = mybir.dt.float32
F32R = mybir.dt.float32r
BF16 = mybir.dt.bfloat16
I32 = mybir.dt.int32
U32 = mybir.dt.uint32
ALU = mybir.AluOpType
ACT = mybir.ActivationFunctionType
AX_X = mybir.AxisListType.X

P = 128
B, S, E = 32, 64, 512
H, KVH, D = 32, 8, 128
T = B * S
HALVES = 2
HT = T // HALVES
TILES = HT // P
HB = B // HALVES
EC = E // P
GROUP = 512
GROUPS = HT // GROUP
GT = GROUP // P
GB = GROUP // S
PAIRS = H // KVH // 2
TICKS = PAIRS * GROUPS
EXPERTS, RANK, TOP_K, ROUTER = 64, 8, 16, 16
N_B = EXPERTS * RANK
FFN_SCALE = 32 / TOP_K
MAX_POS = 512
MASKED = -1.0e30
REMOVED = -3.0e38
EPS = 1e-5
SM_SCALE = 1.0 / float(D) ** 0.5

PROJ = GROUPS + 2 * TICKS
YT = TICKS * GT
NIT = HALVES * KVH
POS_STEPS = 4
MOMENT_STEPS = 6
TRIG_COPIES = 2 * TILES // 4
GATE_STEPS = 6


def u_of(s):
    return [GROUPS + 2 * s, GROUPS + 2 * s + 1]


def tick_of(u):
    return divmod(u - GROUPS, 2)


U_ORDER_K = [*range(GROUPS), *u_of(0)]


def token_group(u):
    return u if u < GROUPS else tick_of(u)[0] % GROUPS


def flamingo_block(nc, x, ctx_t, mask, pos, gains, wq, wo, wkv, a_t, b_t, router_t, keys_t, rope, ident, out):
    with ExitStack() as stack:
        def sb(name, shape, dt=F32):
            return stack.enter_context(nc.sbuf_tensor(name, shape, dt))

        def bank(name):
            return stack.enter_context(nc.psum_tensor(name, [P, 512], F32))

        def sem(name):
            return stack.enter_context(nc.semaphore(name))

        x_hi = sb("x_hi", [P, EC, HT], F32R)
        x_lo = sb("x_lo", [P, EC, HT], F32R)
        c_hi = sb("c_hi", [P, EC, HT], F32R)
        c_lo = sb("c_lo", [P, EC, HT], F32R)
        resid = sb("resid", [P, HALVES * TILES, E])
        mask_bias = sb("mask_bias", [P, HB, S], BF16)
        cos_t = sb("cos_t", [P, HT])
        sin_t = sb("sin_t", [P, HT])
        wq_hi = sb("wq_hi", [P, PAIRS, EC, 2 * D], F32R)
        wq_lo = sb("wq_lo", [P, PAIRS, EC, 2 * D], F32R)
        wo_hi = sb("wo_hi", [P, PAIRS, 2, E], F32R)
        wo_lo = sb("wo_lo", [P, PAIRS, 2, E], F32R)
        wkv_hi = sb("wkv_hi", [P, 2, EC, D], F32R)
        wkv_lo = sb("wkv_lo", [P, 2, EC, D], F32R)
        wq_raw = sb("wq_raw", [P, PAIRS, EC * 2 * D])
        wo_raw = sb("wo_raw", [P, PAIRS, 2 * E])
        wkv_raw = sb("wkv_raw", [P, 2 * EC * D])
        k_rot = sb("k_rot", [P, HT])
        v_tok = sb("v_tok", [P, TILES, D])
        swapped = sb("swapped", [P, 2, GROUP])
        straight = sb("straight", [P, 2, GROUP])
        q_rot = sb("q_rot", [P, GB, 2, S])
        score = sb("score", [P, GB, S])
        expo = sb("expo", [P, GB, S])
        prob = sb("prob", [P, GB, S])
        prob_t = sb("prob_t", [P, 512])
        o_hi = sb("o_hi", [P, 2, GROUP], F32R)
        o_lo = sb("o_lo", [P, 2, GROUP], F32R)
        eye = sb("eye", [P, P])
        row_max = sb("row_max", [P, GB])
        row_sum = sb("row_sum", [P, GB])
        row_inv = sb("row_inv", [P, GB])
        stats = sb("stats", [P, TILES, 6])
        mean = sb("mean", [P, TILES])
        gap = sb("gap", [P, TILES])
        var_eps = sb("var_eps", [P, TILES])
        std = sb("std", [P, TILES])
        rstd = sb("rstd", [P, TILES])
        gain = sb("gain", [P, 2])
        gate_gain = sb("gate_gain", [P, 3])
        pos_i = sb("pos_i", [P, TILES], I32)
        pos_f = sb("pos_f", [P, TILES])
        pos_w = sb("pos_w", [P, TILES])
        pos_u = sb("pos_u", [P, TILES], U32)
        keys_sb = sb("keys_sb", [ROUTER, EXPERTS])
        top_a = sb("top_a", [P, TILES, 8])
        top_b = sb("top_b", [P, TILES, 8])

        proj_ps = [bank("proj_ps0"), bank("proj_ps1")]
        score_ps = bank("score_ps")
        prob_ps = bank("prob_ps")
        attn_ps = [bank("attn_ps0"), bank("attn_ps1")]
        y_ps = [bank("y_ps0"), bank("y_ps1")]

        x_landed = [sem("x_landed0"), sem("x_landed1")]
        ctx_landed = [sem("ctx_landed0"), sem("ctx_landed1")]
        mask_landed = sem("mask_landed")
        pos_landed = sem("pos_landed")
        small_landed = sem("small_landed")
        wkv_landed = sem("wkv_landed")
        wq_landed = [sem("wq_landed0"), sem("wq_landed1")]
        wo_landed = [sem("wo_landed0"), sem("wo_landed1")]
        rope_landed = [sem(f"rope_landed{i}") for i in range(4)]
        a_landed = sem("a_landed")
        b_landed = sem("b_landed")
        router_landed = sem("router_landed")
        out_stored = [sem("out_stored0"), sem("out_stored1")]
        waits_passed = sem("waits_passed")
        wkv_hi_ready = sem("wkv_hi_ready")
        wkv_lo_ready = sem("wkv_lo_ready")
        wq_hi_ready = [sem("wq_hi_ready0"), sem("wq_hi_ready1")]
        wq_lo_ready = [sem("wq_lo_ready0"), sem("wq_lo_ready1")]
        wo_hi_ready = [sem("wo_hi_ready0"), sem("wo_hi_ready1")]
        wo_lo_ready = [sem("wo_lo_ready0"), sem("wo_lo_ready1")]
        ctx_hi_ready = sem("ctx_hi_ready")
        ctx_lo_ready = sem("ctx_lo_ready")
        ffn_hi_ready = sem("ffn_hi_ready")
        ffn_lo_ready = sem("ffn_lo_ready")
        stats_ready = sem("stats_ready")
        moment_step = sem("moment_step")
        var_ready = sem("var_ready")
        std_ready = sem("std_ready")
        rstd_ready = sem("rstd_ready")
        normed = sem("normed")
        x_turned = sem("x_turned")
        x_hi_ready = sem("x_hi_ready")
        x_lo_ready = sem("x_lo_ready")
        tanh_ready = sem("tanh_ready")
        gain_ready = sem("gain_ready")
        pos_step = sem("pos_step")
        trig_turned = sem("trig_turned")
        trig_ready = sem("trig_ready")
        bias_ready = sem("bias_ready")
        proj_done = sem("proj_done")
        swap_done = sem("swap_done")
        cos_done = sem("cos_done")
        sin_done = sem("sin_done")
        rope_done = sem("rope_done")
        v_done = sem("v_done")
        v_copied = sem("v_copied")
        scores_done = sem("scores_done")
        masked_done = sem("masked_done")
        max_done = sem("max_done")
        shift_done = sem("shift_done")
        exp_done = sem("exp_done")
        sum_done = sem("sum_done")
        inv_done = sem("inv_done")
        probs_done = sem("probs_done")
        probs_turned = sem("probs_turned")
        probs_copied = sem("probs_copied")
        attn_done = sem("attn_done")
        o_hi_ready = sem("o_hi_ready")
        o_lo_ready = sem("o_lo_ready")
        y_done = sem("y_done")
        y_added = sem("y_added")
        route_done = sem("route_done")
        route_copied = sem("route_copied")
        logits_done = sem("logits_done")
        logits_copied = sem("logits_copied")
        topk_step = sem("topk_step")
        gate_exp = sem("gate_exp")
        gate_step = sem("gate_step")
        z_done = sem("z_done")
        z_gated = sem("z_gated")
        z_turned = sem("z_turned")
        z_hi_ready = sem("z_hi_ready")
        z_lo_ready = sem("z_lo_ready")
        ffn_done = sem("ffn_done")
        final_done = sem("final_done")

        ctx_raw = [k_rot[:, :], v_tok[:, :, :].rearrange("p t d -> p (t d)")]
        mask_raw = q_rot[:, :, :, :].rearrange("p b h q -> p (b h q)").bitcast(I32)
        trig_rows = straight[:, :, :].rearrange("p s (u w) -> p (s u) w", w=2 * D)
        prob_t_v = prob_t[:, :]
        attn_v = [a[:, :].rearrange("p (t h q) -> p t h q", t=GT, h=2) for a in attn_ps]
        o_hi_v = o_hi[:, :, :].rearrange("p h (t b q) -> p b t h q", t=GT, b=2)
        o_lo_v = o_lo[:, :, :].rearrange("p h (t b q) -> p b t h q", t=GT, b=2)
        score_v = score[:, :, :].rearrange("p b k -> p (b k)")
        a_hi, a_lo = c_hi[:, :, 0:N_B], c_lo[:, :, 0:N_B]
        b_hi, b_lo = c_hi[:, :, N_B:N_B + E], c_lo[:, :, N_B:N_B + E]
        a_raw = wq_raw[:, :, :].rearrange("p a (c n) -> p (a c) n", n=N_B)
        b_raw = wo_raw[:, :, :].rearrange("p a (c n) -> p (a c) n", n=E)
        router_raw = wkv_raw[:, 0:EC * P].rearrange("p (c n) -> p c n", c=EC)
        router_hi, router_lo = wkv_hi[:, 0, :, :], wkv_lo[:, 0, :, :]
        route = k_rot[0:ROUTER, :]
        logits, struck, weight, gate = score, expo, prob, prob_t[:, :].rearrange("p (t e) -> p t e", e=EXPERTS)
        tile_out = q_rot[:, :, :, :].rearrange("p (s b) h q -> p s (b h q)", s=2)

        ffn_splits = [(router_lo, router_raw, router_hi), (a_lo, a_raw, a_hi), (b_lo, b_raw, b_hi)]

        def flat(w):
            return w[:, :, :, :].rearrange("p k c n -> p (k c n)")

        def per_row(ap, n):
            return ap.unsqueeze(2).to_broadcast([P, ap.shape[1], n])

        def wait_alone(engine, semaphore, value):
            engine.wait_ge(semaphore, value)
            engine.sem_inc(waits_passed, 1)

        block = stack.enter_context(nc.Block())

        @block.sync
        def _(sp):
            with sp.Fori(0, HALVES) as half:
                tile0, token0, mask0 = sp.snap(half * TILES), sp.snap(half * HT), sp.snap(half * (HB * S))
                for i in range(2):
                    sp.dma_start(resid[:, bass.ds(half * TILES + i * GT, GT), :],
                                 x[:, bass.ds(half * TILES + i * GT, GT), :]).then_inc(x_landed[i], 16)
                wait_alone(sp, pos_step, half * POS_STEPS)
                sp.dma_start(pos_i[:, :], pos[:, bass.ds(tile0, TILES)]).then_inc(pos_landed, 16)
                sp.wait_ge(scores_done, half * (KVH * TICKS))
                sp.wait_ge(attn_done, half * (KVH * TICKS))
                for c in range(EC):
                    if c >= 2:
                        sp.wait_ge(ctx_hi_ready, half * EC + (c - 1))
                        sp.wait_ge(ctx_lo_ready, half * EC + (c - 1))
                    sp.dma_start(ctx_raw[c % 2],
                                 ctx_t[c * P:(c + 1) * P, bass.ds(token0, HT)]).then_inc(ctx_landed[c % 2], 16)
                    if c == 1:
                        for r in range(2):
                            sp.dma_start(mask_raw[r * S:(r + 1) * S, :],
                                         mask[:, bass.ds(mask0, HB * S)]).then_inc(mask_landed, 16)
                with sp.Fori(0, KVH) as g:
                    it = half * KVH + g
                    pair_row = [sp.snap((g * PAIRS + pair) * P) for pair in range(PAIRS)]
                    g_next = (g + 1) % KVH
                    wkv_row, wq_row = sp.snap(g_next * P), sp.snap(g_next * (PAIRS * P))
                    sp.wait_ge(wq_hi_ready[1], it)
                    sp.wait_ge(wq_lo_ready[1], it)
                    sp.dma_start(wq_raw[:, 1, :], wq[bass.ds(pair_row[1], P), :]).then_inc(wq_landed[1], 16)
                    for pair in range(PAIRS):
                        sp.wait_ge(wo_hi_ready[pair], it)
                        sp.wait_ge(wo_lo_ready[pair], it)
                        sp.dma_start(wo_raw[:, pair, :],
                                     wo[bass.ds(pair_row[pair], P), :]).then_inc(wo_landed[pair], 16)
                    sp.wait_ge(wkv_hi_ready, it + 1)
                    sp.wait_ge(wkv_lo_ready, it + 1)
                    sp.dma_start(wkv_raw[:, :], wkv[bass.ds(wkv_row, P), :]).then_inc(wkv_landed, 16)
                    sp.wait_ge(wq_hi_ready[0], it + 1)
                    sp.wait_ge(wq_lo_ready[0], it + 1)
                    sp.dma_start(wq_raw[:, 0, :], wq[bass.ds(wq_row, P), :]).then_inc(wq_landed[0], 16)
            for pair in range(PAIRS):
                sp.wait_ge(wq_hi_ready[pair], NIT + 1 - pair)
                sp.wait_ge(wq_lo_ready[pair], NIT + 1 - pair)
                sp.wait_ge(wo_hi_ready[pair], NIT)
                sp.wait_ge(wo_lo_ready[pair], NIT)
            sp.wait_ge(wkv_hi_ready, NIT + 1)
            sp.wait_ge(wkv_lo_ready, NIT + 1)
            sp.dma_start(router_raw, router_t).then_inc(router_landed, 16)
            sp.dma_start(a_raw, a_t).then_inc(a_landed, 16)
            sp.dma_start(b_raw, b_t).then_inc(b_landed, 16)
            with sp.Fori(0, HALVES) as half:
                for t in range(TILES):
                    tile = sp.snap(half * TILES + t)
                    sp.wait_ge(final_done, half * TILES + t + 1)
                    sp.dma_start(out[:, bass.ds(tile, 1), :],
                                 tile_out[:, t % 2:t % 2 + 1, :]).then_inc(out_stored[t % 2], 16)
            for s in out_stored:
                sp.wait_ge(s, 16 * (HALVES * TILES // 2))

        @block.gpsimd
        def _(pool):
            def weights_lo(lo, raw, hi, hi_ready, lo_ready, n):
                pool.wait_ge(hi_ready, n)
                nc.gpsimd.tensor_tensor(lo, raw, hi.bitcast(F32), ALU.subtract).then_inc(lo_ready, 1)

            def wkv_part(n):
                weights_lo(flat(wkv_lo), wkv_raw[:, :], flat(wkv_hi), wkv_hi_ready, wkv_lo_ready, n)

            def wq_part(pair, n):
                weights_lo(wq_lo[:, pair].rearrange("p c n -> p (c n)"), wq_raw[:, pair, :],
                           wq_hi[:, pair].rearrange("p c n -> p (c n)"), wq_hi_ready[pair], wq_lo_ready[pair], n)

            def wo_part(pair, n):
                weights_lo(wo_lo[:, pair].rearrange("p c n -> p (c n)"), wo_raw[:, pair, :],
                           wo_hi[:, pair].rearrange("p c n -> p (c n)"), wo_hi_ready[pair], wo_lo_ready[pair], n)

            def gather(half, t):
                if t >= 4:
                    wait_alone(pool, trig_turned, half * TILES + (t - 3))
                pool.indirect_dma_start(out=trig_rows[:, t % 4, :], out_offset=None, in_=rope,
                                        in_offset=bass.IndirectOffsetOnAxis(ap=pos_u[:, t:t + 1], axis=0)
                                        ).then_inc(rope_landed[t % 4], 16)

            wkv_part(1)
            wq_part(0, 1)
            with pool.Fori(0, HALVES) as half:
                pool.wait_ge(rope_done, half * (KVH * PROJ))
                wait_alone(pool, pos_step, half * POS_STEPS + POS_STEPS)
                for t in range(4):
                    gather(half, t)
                for c in range(EC):
                    pool.wait_ge(ctx_hi_ready, half * EC + (c + 1))
                    nc.gpsimd.tensor_tensor(c_lo[:, c, :], ctx_raw[c % 2], c_hi[:, c, :].bitcast(F32),
                                            ALU.subtract).then_inc(ctx_lo_ready, 1)
                for t in range(4, TILES):
                    gather(half, t)
                with pool.Fori(0, KVH) as g:
                    it = half * KVH + g

                    def times_sin(u):
                        pool.wait_ge(swap_done, it * PROJ + (u + 1))
                        c = token_group(u) * GROUP
                        nc.gpsimd.tensor_tensor(swapped[:, u % 2, :], swapped[:, u % 2, :],
                                                sin_t[:, c:c + GROUP], ALU.mult).then_inc(sin_done, 1)

                    pool.wait_ge(trig_ready, half * TRIG_COPIES + TRIG_COPIES)
                    for u in U_ORDER_K:
                        times_sin(u)
                    for s in range(TICKS):
                        if s == 0:
                            wq_part(1, it + 1)
                            wo_part(0, it + 1)
                        if s < TICKS - 1:
                            for u in u_of(s + 1):
                                times_sin(u)
                        if s == 1:
                            wo_part(1, it + 1)
                        if s == 2:
                            wkv_part(it + 2)
                            wq_part(0, it + 2)
            for n, (lo, raw, hi) in enumerate(ffn_splits):
                pool.wait_ge(ffn_hi_ready, n + 1)
                nc.gpsimd.tensor_tensor(lo, raw, hi.bitcast(F32), ALU.subtract).then_inc(ffn_lo_ready, 1)

        @block.scalar
        def _(act):
            def weights_hi(hi, raw, landed, ready, n):
                act.wait_ge(landed, 16 * n)
                nc.scalar.copy(hi, raw).then_inc(ready, 1)

            def wkv_part(n):
                weights_hi(flat(wkv_hi), wkv_raw[:, :], wkv_landed, wkv_hi_ready, n)

            def wq_part(pair, n):
                weights_hi(wq_hi[:, pair].rearrange("p c n -> p (c n)"), wq_raw[:, pair, :],
                           wq_landed[pair], wq_hi_ready[pair], n)

            def wo_part(pair, n):
                weights_hi(wo_hi[:, pair].rearrange("p c n -> p (c n)"), wo_raw[:, pair, :],
                           wo_landed[pair], wo_hi_ready[pair], n)

            def turned_hi(n0, t):
                act.wait_ge(x_turned, n0 + (t + 1))
                nc.scalar.copy(x_hi[:, :, t * P:(t + 1) * P],
                               proj_ps[t % 2][:, :].rearrange("p (c n) -> p c n", c=EC)).then_inc(x_hi_ready, 1)

            act.dma_start(wkv_raw[:, :], wkv[0:P, :]).then_inc(wkv_landed, 16)
            act.dma_start(wq_raw[:, 0, :], wq[0:P, :]).then_inc(wq_landed[0], 16)
            act.dma_start(eye[:, :], ident).then_inc(small_landed, 16)
            act.dma_start(gain[:, :], gains).then_inc(small_landed, 16)
            act.dma_start(keys_sb[:, :], keys_t).then_inc(small_landed, 16)
            act.wait_ge(small_landed, 48)
            nc.scalar.activation(gate_gain[:, 0:2], gain[:, :], ACT.Tanh).then_inc(tanh_ready, 1)
            wkv_part(1)
            wq_part(0, 1)
            with act.Fori(0, HALVES) as half:
                for c in range(EC):
                    act.wait_ge(ctx_landed[c % 2], half * (16 * EC // 2) + 16 * (c // 2 + 1))
                    if c == 0:
                        act.wait_ge(v_done, half * (2 * KVH))
                        act.wait_ge(proj_done, half * (PROJ * KVH))
                    nc.scalar.copy(c_hi[:, c, :], ctx_raw[c % 2]).then_inc(ctx_hi_ready, 1)
                act.wait_ge(var_ready, half + 1)
                nc.scalar.activation(std[:, :], var_eps[:, :], ACT.Sqrt).then_inc(std_ready, 1)
                for t in range(TILES):
                    turned_hi(half * TILES, t)
                act.wait_ge(cos_done, half * (PROJ * KVH))
                act.wait_ge(sin_done, half * (PROJ * KVH))
                for r in range(TILES // 4):
                    act.wait_ge(trig_turned, half * TILES + 4 * (r + 1))
                    nc.scalar.copy(cos_t[:, r * 512:(r + 1) * 512], score_ps[:, :]).then_inc(trig_ready, 1)
                    nc.scalar.copy(sin_t[:, r * 512:(r + 1) * 512], prob_ps[:, :]).then_inc(trig_ready, 1)
                with act.Fori(0, KVH) as g:
                    it = half * KVH + g
                    tick0 = it * TICKS

                    def swap(u):
                        act.wait_ge(proj_done, it * PROJ + (u + 1))
                        act.wait_ge(rope_done, it * PROJ + max(u - 1, 0))
                        ps = proj_ps[u % 2]
                        nc.scalar.copy(swapped[0:D // 2, u % 2, :], ps[D // 2:D, :])
                        nc.scalar.copy(swapped[D // 2:D, u % 2, :], ps[0:D // 2, :]).then_inc(swap_done, 1)

                    for u in U_ORDER_K:
                        swap(u)
                    act.wait_ge(proj_done, it * PROJ)
                    wq_part(1, it + 1)
                    act.wait_ge(y_done, it * YT)
                    wo_part(0, it + 1)
                    for s in range(TICKS):
                        act.wait_ge(shift_done, tick0 + (s + 1))
                        act.wait_ge(probs_done, tick0 + s)
                        nc.scalar.activation(expo[:, :, :], score[:, :, :], ACT.Exp, scale=SM_SCALE).then_inc(exp_done, 1)
                        if s < TICKS - 1:
                            for u in u_of(s + 1):
                                swap(u)
                        if s == 1:
                            wo_part(1, it + 1)
                        if s == 2:
                            act.wait_ge(v_done, it * 2 + 2)
                            wkv_part(it + 2)
                            act.wait_ge(proj_done, it * PROJ + (u_of(GROUPS - 1)[-1] + 1))
                            wq_part(0, it + 2)
                        act.wait_ge(probs_turned, tick0 + (s + 1))
                        act.wait_ge(attn_done, tick0 + s)
                        nc.scalar.copy(prob_t[:, :], prob_ps[:, :]).then_inc(probs_copied, 1)
                        act.wait_ge(attn_done, tick0 + (s + 1))
                        act.wait_ge(y_done, (tick0 + s) * GT)
                        for b in range(2):
                            nc.scalar.copy(o_hi_v[:, b], attn_v[b]).then_inc(o_hi_ready, 1)
            act.wait_ge(proj_done, NIT * PROJ)
            act.wait_ge(v_done, NIT * 2)
            for n, (lo, raw, hi) in enumerate(ffn_splits):
                act.wait_ge([router_landed, a_landed, b_landed][n], 16)
                nc.scalar.copy(hi, raw).then_inc(ffn_hi_ready, 1)
            with act.Fori(0, HALVES) as half:
                act.wait_ge(var_ready, half + (HALVES + 1))
                nc.scalar.activation(std[:, :], var_eps[:, :], ACT.Sqrt).then_inc(std_ready, 1)
                act.wait_ge(z_done, half * TILES)
                for t in range(TILES):
                    turned_hi(half * TILES + HALVES * TILES, t)
                act.wait_ge(logits_done, half)
                for c in range(GROUPS):
                    act.wait_ge(route_done, half * GROUPS + (c + 1))
                    nc.scalar.copy(route[:, c * GROUP:(c + 1) * GROUP],
                                   attn_ps[c][0:ROUTER, :]).then_inc(route_copied, 1)
                act.wait_ge(gate_step, half * GATE_STEPS + 1)
                nc.scalar.activation(weight[:, :, :], weight[:, :, :], ACT.Exp).then_inc(gate_exp, 1)
                for t in range(TILES):
                    act.wait_ge(z_turned, half * TILES + (t + 1))
                    if t >= 2:
                        act.wait_ge(ffn_done, half * TILES + (t - 1))
                    else:
                        act.wait_ge(ffn_done, half * TILES)
                    nc.scalar.copy(o_hi[:, t % 2, :], prob_ps[:, :]).then_inc(z_hi_ready, 1)

        @block.vector
        def _(dve):
            def layer_norm(half, n):
                for t in range(TILES):
                    nc.vector.bn_stats(stats[:, t, :], resid[:, bass.ds(half * TILES + t, 1), :]
                                       .rearrange("p a e -> p (a e)")).then_inc(stats_ready, 1)
                mean_a, mean_b = stats[:, :, 1], stats[:, :, 4]
                dve.wait_ge(stats_ready, n * TILES + TILES)
                nc.vector.tensor_tensor(mean[:, :], mean_a, mean_b, ALU.add).then_inc(moment_step, 1)
                nc.vector.tensor_tensor(gap[:, :], mean_a, mean_b, ALU.subtract).then_inc(moment_step, 1)
                nc.vector.tensor_tensor(var_eps[:, :], stats[:, :, 2], stats[:, :, 5], ALU.add).then_inc(moment_step, 1)
                dve.wait_ge(moment_step, n * MOMENT_STEPS + 3)
                nc.vector.tensor_scalar(mean[:, :], mean[:, :], 0.5, None, ALU.mult).then_inc(moment_step, 1)
                nc.vector.tensor_tensor(gap[:, :], gap[:, :], gap[:, :], ALU.mult).then_inc(moment_step, 1)
                nc.vector.tensor_scalar(var_eps[:, :], var_eps[:, :], 1.0 / E, EPS, ALU.mult, ALU.add).then_inc(moment_step, 1)
                dve.wait_ge(moment_step, n * MOMENT_STEPS + 6)
                nc.vector.scalar_tensor_tensor(out=var_eps[:, :], in0=gap[:, :], scalar=0.25, in1=var_eps[:, :],
                                               op0=ALU.mult, op1=ALU.add).then_inc(var_ready, 1)
                dve.wait_ge(std_ready, n + 1)
                nc.vector.reciprocal(rstd[:, :], std[:, :]).then_inc(rstd_ready, 1)
                dve.wait_ge(rstd_ready, n + 1)

                def normalise(t):
                    if t >= 2:
                        dve.wait_ge(x_turned, n * TILES + (t - 1))
                    nc.vector.tensor_scalar(swapped[:, t % 2, :], resid[:, bass.ds(half * TILES + t, 1), :]
                                            .rearrange("p a e -> p (a e)"), mean[:, t:t + 1], rstd[:, t:t + 1],
                                            ALU.subtract, ALU.mult).then_inc(normed, 1)

                normalise(0)
                for t in range(TILES):
                    if t + 1 < TILES:
                        normalise(t + 1)
                    dve.wait_ge(x_hi_ready, n * TILES + (t + 1))
                    nc.vector.tensor_tensor(x_lo[:, :, t * P:(t + 1) * P],
                                            proj_ps[t % 2][:, :].rearrange("p (c n) -> p c n", c=EC),
                                            x_hi[:, :, t * P:(t + 1) * P].bitcast(F32),
                                            ALU.subtract).then_inc(x_lo_ready, 1)

            dve.wait_ge(tanh_ready, 1)
            nc.vector.tensor_scalar(gate_gain[:, 2:3], gate_gain[:, 1:2], FFN_SCALE, None, ALU.mult).then_inc(gain_ready, 1)
            with dve.Fori(0, HALVES) as half:
                dve.wait_ge(pos_landed, half * 16 + 16)
                step0 = half * POS_STEPS
                nc.vector.tensor_copy(pos_f[:, :], pos_i[:, :]).then_inc(pos_step, 1)
                dve.wait_ge(pos_step, step0 + 1)
                nc.vector.tensor_scalar(pos_w[:, :], pos_f[:, :], 0.0, float(MAX_POS), ALU.is_lt, ALU.mult).then_inc(pos_step, 1)
                dve.wait_ge(pos_step, step0 + 2)
                nc.vector.tensor_tensor(pos_f[:, :], pos_f[:, :], pos_w[:, :], ALU.add).then_inc(pos_step, 1)
                dve.wait_ge(pos_step, step0 + 3)
                if True:
                    for i in range(4):
                        dve.wait_ge(rope_landed[i], half * (16 * TILES // 4))
                nc.vector.tensor_scalar(pos_u[:, :], pos_f[:, :], 0.0, float(MAX_POS - 1), ALU.max, ALU.min).then_inc(pos_step, 1)
                for i in range(2):
                    dve.wait_ge(x_landed[i], half * 16 + 16)
                dve.wait_ge(rope_done, half * (PROJ * KVH))
                dve.wait_ge(proj_done, half * (PROJ * KVH))
                layer_norm(half, half)
                dve.wait_ge(mask_landed, half * 32 + 32)
                dve.wait_ge(masked_done, half * (KVH * TICKS))
                nc.vector.tensor_scalar(mask_bias[:, :, :].rearrange("p b k -> p (b k)"), mask_raw, 0.0, MASKED,
                                        ALU.is_equal, ALU.mult).then_inc(bias_ready, 1)
                dve.wait_ge(bias_ready, half + 1)
                wait_alone(dve, trig_ready, half * TRIG_COPIES + TRIG_COPIES)
                with dve.Fori(0, KVH) as g:
                    it = half * KVH + g
                    tick0 = it * TICKS

                    def times_cos(u):
                        dve.wait_ge(swap_done, it * PROJ + (u + 1))
                        dve.wait_ge(rope_done, it * PROJ + max(u - 1, 0))
                        c = token_group(u) * GROUP
                        nc.vector.tensor_tensor(straight[:, u % 2, :], proj_ps[u % 2][:, :], cos_t[:, c:c + GROUP],
                                                ALU.mult).then_inc(cos_done, 1)

                    def add_rotated(u):
                        dve.wait_ge(cos_done, it * PROJ + (u + 1))
                        dve.wait_ge(sin_done, it * PROJ + (u + 1))
                        if u < GROUPS:
                            dve.wait_ge(scores_done, tick0)
                            dst = k_rot[:, u * GROUP:(u + 1) * GROUP].rearrange("p (b q) -> p b q", q=S)
                        else:
                            s, head = tick_of(u)
                            dve.wait_ge(scores_done, tick0 + s)
                            dst = q_rot[:, :, head, :]
                        nc.vector.tensor_tensor(dst, straight[:, u % 2, :].rearrange("p (b q) -> p b q", q=S),
                                                swapped[:, u % 2, :].rearrange("p (b q) -> p b q", q=S),
                                                ALU.add).then_inc(rope_done, 1)

                    def copy_values(j):
                        dve.wait_ge(v_done, it * 2 + (j + 1))
                        dve.wait_ge(attn_done, tick0)
                        nc.vector.tensor_copy(v_tok[:, j * 4:(j + 1) * 4, :].rearrange("p t d -> p (t d)"),
                                              y_ps[j][:, :]).then_inc(v_copied, 1)

                    def add_output(s):
                        pair, grp = divmod(s, GROUPS)
                        for t in range(GT):
                            dve.wait_ge(y_done, (tick0 + s) * GT + (t + 1))
                            dve.wait_ge(y_added, (tick0 + s) * GT)
                            r = resid[:, bass.ds(half * TILES + (grp * GT + t), 1), :].rearrange("p a e -> p (a e)")
                            nc.vector.scalar_tensor_tensor(out=r, in0=y_ps[t % 2][:, :], scalar=gate_gain[:, 0:1],
                                                           in1=r, op0=ALU.mult, op1=ALU.add).then_inc(y_added, 1)

                    times_cos(0)
                    times_cos(1)
                    add_rotated(0)
                    times_cos(2)
                    add_rotated(1)
                    times_cos(3)
                    add_rotated(2)
                    copy_values(0)
                    add_rotated(3)
                    copy_values(1)
                    for s in range(TICKS):
                        grp = s % GROUPS
                        bias = mask_bias[:, grp * GB:(grp + 1) * GB, :].rearrange("p b k -> p (b k)")
                        dve.wait_ge(scores_done, tick0 + (s + 1))
                        dve.wait_ge(exp_done, tick0 + s)
                        nc.vector.tensor_tensor(score_v, score_ps[:, :], bias, ALU.add).then_inc(masked_done, 1)
                        dve.wait_ge(masked_done, tick0 + (s + 1))
                        nc.vector.reduce_max(row_max[:, :], score[:, :, :], AX_X).then_inc(max_done, 1)
                        dve.wait_ge(max_done, tick0 + (s + 1))
                        nc.vector.tensor_tensor(score[:, :, :], score[:, :, :], per_row(row_max[:, :], S),
                                                ALU.subtract).then_inc(shift_done, 1)
                        if s < TICKS - 1:
                            times_cos(u_of(s + 1)[0])
                        dve.wait_ge(exp_done, tick0 + (s + 1))
                        nc.vector.reduce_sum(row_sum[:, :], expo[:, :, :], AX_X).then_inc(sum_done, 1)
                        dve.wait_ge(sum_done, tick0 + (s + 1))
                        nc.vector.reciprocal(row_inv[:, :], row_sum[:, :]).then_inc(inv_done, 1)
                        dve.wait_ge(inv_done, tick0 + (s + 1))
                        dve.wait_ge(probs_turned, tick0 + s)
                        nc.vector.tensor_tensor(prob[:, :, :], expo[:, :, :], per_row(row_inv[:, :], S),
                                                ALU.mult).then_inc(probs_done, 1)
                        if s < TICKS - 1:
                            add_rotated(u_of(s + 1)[0])
                            times_cos(u_of(s + 1)[1])
                            add_rotated(u_of(s + 1)[1])
                        if s >= 1:
                            add_output(s - 1)
                        dve.wait_ge(y_done, (tick0 + s) * GT)
                        for b in range(2):
                            dve.wait_ge(o_hi_ready, (tick0 + s) * 2 + (b + 1))
                            nc.vector.tensor_tensor(o_lo_v[:, b], attn_v[b], o_hi_v[:, b].bitcast(F32),
                                                    ALU.subtract).then_inc(o_lo_ready, 1)
                    add_output(TICKS - 1)
            dve.wait_ge(y_added, NIT * YT)
            dve.wait_ge(rope_done, NIT * PROJ)
            dve.wait_ge(gain_ready, 1)
            with dve.Fori(0, HALVES) as half:
                dve.wait_ge(z_done, half * TILES)
                layer_norm(half, half + HALVES)
                dve.wait_ge(logits_done, half + 1)
                dve.wait_ge(z_gated, half * TILES)
                nc.vector.tensor_copy(score_v, score_ps[:, :]).then_inc(logits_copied, 1)
                wait_alone(dve, logits_copied, half + 1)
                steps = half * (4 * TILES)
                for t in range(TILES):
                    nc.vector.max(top_a[:, t, :], logits[:, t, :]).then_inc(topk_step, 1)
                wait_alone(dve, topk_step, steps + TILES)
                for t in range(TILES):
                    nc.vector.match_replace(struck[:, t, :], top_a[:, t, :], logits[:, t, :], REMOVED).then_inc(topk_step, 1)
                wait_alone(dve, topk_step, steps + 2 * TILES)
                for t in range(TILES):
                    nc.vector.max(top_b[:, t, :], struck[:, t, :]).then_inc(topk_step, 1)
                wait_alone(dve, topk_step, steps + 3 * TILES)
                for t in range(TILES):
                    nc.vector.match_replace(struck[:, t, :], top_b[:, t, :], struck[:, t, :], REMOVED).then_inc(topk_step, 1)
                dve.wait_ge(topk_step, steps + 4 * TILES)
                gates0 = half * GATE_STEPS
                nc.vector.tensor_tensor(weight[:, :, :], logits[:, :, :], top_a[:, :, 0:1].to_broadcast([P, TILES, EXPERTS]),
                                        ALU.subtract).then_inc(gate_step, 1)
                dve.wait_ge(gate_step, gates0 + 1)
                nc.vector.tensor_tensor(struck[:, :, :], struck[:, :, :], logits[:, :, :], ALU.not_equal).then_inc(gate_step, 1)
                dve.wait_ge(gate_step, gates0 + 2)
                dve.wait_ge(gate_exp, half + 1)
                nc.vector.tensor_tensor(weight[:, :, :], weight[:, :, :], struck[:, :, :], ALU.mult).then_inc(gate_step, 1)
                dve.wait_ge(gate_step, gates0 + 3)
                nc.vector.reduce_sum(row_sum[:, :], weight[:, :, :], AX_X).then_inc(gate_step, 1)
                dve.wait_ge(gate_step, gates0 + 4)
                nc.vector.reciprocal(row_inv[:, :], row_sum[:, :]).then_inc(gate_step, 1)
                dve.wait_ge(gate_step, gates0 + 5)
                nc.vector.tensor_tensor(gate, weight[:, :, :], per_row(row_inv[:, :], EXPERTS), ALU.mult).then_inc(gate_step, 1)
                dve.wait_ge(gate_step, gates0 + 6)

                def gate_z(t):
                    dve.wait_ge(z_done, half * TILES + (t + 1))
                    dve.wait_ge(z_turned, half * TILES + max(t - 1, 0))
                    nc.vector.tensor_tensor(straight[:, t % 2, :].rearrange("p (e r) -> p e r", r=RANK),
                                            proj_ps[t % 2][:, :].rearrange("p (e r) -> p e r", r=RANK),
                                            per_row(gate[:, t, :], RANK), ALU.mult).then_inc(z_gated, 1)

                gate_z(0)
                for t in range(TILES):
                    if t + 1 < TILES:
                        gate_z(t + 1)
                    dve.wait_ge(z_hi_ready, half * TILES + (t + 1))
                    dve.wait_ge(ffn_done, half * TILES + max(t - 1, 0))
                    nc.vector.tensor_tensor(o_lo[:, t % 2, :], prob_ps[:, :], o_hi[:, t % 2, :].bitcast(F32),
                                            ALU.subtract).then_inc(z_lo_ready, 1)
                    dve.wait_ge(ffn_done, half * TILES + (t + 1))
                    dve.wait_ge(out_stored[t % 2], half * (8 * TILES) + 16 * (t // 2))
                    nc.vector.scalar_tensor_tensor(out=tile_out[:, t % 2, :], in0=y_ps[t % 2][:, :],
                                                   scalar=gate_gain[:, 2:3],
                                                   in1=resid[:, bass.ds(half * TILES + t, 1), :].rearrange("p a e -> p (a e)"),
                                                   op0=ALU.mult, op1=ALU.add).then_inc(final_done, 1)

        @block.tensor
        def _(pe):
            def turn_tokens(n):
                for t in range(TILES):
                    pe.wait_ge(normed, n * TILES + (t + 1))
                    if t >= 2:
                        pe.wait_ge(x_lo_ready, n * TILES + (t - 1))
                    for c in range(EC):
                        last = nc.tensor.transpose(proj_ps[t % 2][:, c * P:(c + 1) * P],
                                                   swapped[:, t % 2, c * P:(c + 1) * P], eye[:, :])
                    last.then_inc(x_turned, 1)

            def three_products(ps, parts):
                n = len(parts)
                for i, (l_hi, l_lo, r_hi, r_lo) in enumerate(parts):
                    nc.tensor.matmul(ps, l_hi, r_hi, start=(i == 0), stop=False)
                    nc.tensor.matmul(ps, l_hi, r_lo, start=False, stop=False)
                    last = nc.tensor.matmul(ps, l_lo, r_hi, start=False, stop=(i == n - 1))
                return last

            pe.wait_ge(small_landed, 48)
            with pe.Fori(0, HALVES) as half:
                pe.wait_ge(swap_done, half * (KVH * PROJ))
                pe.wait_ge(cos_done, half * (KVH * PROJ))
                turn_tokens(half)
                pe.wait_ge(masked_done, half * (KVH * TICKS))
                pe.wait_ge(probs_copied, half * (KVH * TICKS))
                for t in range(TILES):
                    pe.wait_ge(rope_landed[t % 4], half * (16 * TILES // 4) + 16 * (t // 4 + 1))
                    if t == 4:
                        pe.wait_ge(trig_ready, half * TRIG_COPIES + 2)
                    c = (t % 4) * P
                    nc.tensor.transpose(score_ps[:, c:c + P], trig_rows[:, t % 4, 0:D], eye[:, :])
                    nc.tensor.transpose(prob_ps[:, c:c + P], trig_rows[:, t % 4, D:2 * D], eye[:, :]).then_inc(trig_turned, 1)
                pe.wait_ge(x_hi_ready, half * TILES + TILES)
                pe.wait_ge(x_lo_ready, half * TILES + TILES)
                pe.wait_ge(ctx_hi_ready, half * EC + EC)
                pe.wait_ge(ctx_lo_ready, half * EC + EC)
                wait_alone(pe, trig_ready, half * TRIG_COPIES + TRIG_COPIES)
                with pe.Fori(0, KVH) as g:
                    it = half * KVH + g
                    tick0 = it * TICKS

                    def bank_free(u):
                        pe.wait_ge(cos_done, it * PROJ + max(u - 1, 0))

                    def project_queries(s):
                        pair, grp = divmod(s, GROUPS)
                        cols = slice(grp * GROUP, (grp + 1) * GROUP)
                        n = it + 1
                        pe.wait_ge(wq_hi_ready[pair], n)
                        pe.wait_ge(wq_lo_ready[pair], n)
                        for head, u in enumerate(u_of(s)):
                            bank_free(u)
                            d = slice(head * D, (head + 1) * D)
                            three_products(proj_ps[u % 2][:, :], [
                                (wq_hi[:, pair, c, d], wq_lo[:, pair, c, d], x_hi[:, c, cols], x_lo[:, c, cols])
                                for c in range(EC)]).then_inc(proj_done, 1)

                    def project_output(s):
                        pair, grp = divmod(s, GROUPS)
                        pe.wait_ge(wo_hi_ready[pair], it + 1)
                        pe.wait_ge(wo_lo_ready[pair], it + 1)
                        pe.wait_ge(o_hi_ready, (tick0 + s + 1) * 2)
                        pe.wait_ge(o_lo_ready, (tick0 + s + 1) * 2)
                        for t in range(GT):
                            n = s * GT + t
                            pe.wait_ge(y_added, it * YT + max(n - 1, 0))
                            tok = slice(t * P, (t + 1) * P)
                            three_products(y_ps[t % 2][:, :], [
                                (o_hi[:, h, tok], o_lo[:, h, tok], wo_hi[:, pair, h, :], wo_lo[:, pair, h, :])
                                for h in range(2)]).then_inc(y_done, 1)

                    pe.wait_ge(wkv_hi_ready, it + 1)
                    pe.wait_ge(wkv_lo_ready, it + 1)
                    for u in range(GROUPS):
                        bank_free(u)
                        cols = slice(u * GROUP, (u + 1) * GROUP)
                        three_products(proj_ps[u][:, :], [
                            (wkv_hi[:, 0, c, :], wkv_lo[:, 0, c, :], c_hi[:, c, cols], c_lo[:, c, cols])
                            for c in range(EC)]).then_inc(proj_done, 1)
                    project_queries(0)
                    pe.wait_ge(y_added, it * YT)
                    for j in range(2):
                        for t in range(4):
                            tok = slice((j * 4 + t) * P, (j * 4 + t + 1) * P)
                            last = three_products(y_ps[j][:, t * D:(t + 1) * D], [
                                (c_hi[:, c, tok], c_lo[:, c, tok], wkv_hi[:, 1, c, :], wkv_lo[:, 1, c, :])
                                for c in range(EC)])
                        last.then_inc(v_done, 1)
                    for s in range(TICKS):
                        grp = s % GROUPS
                        pe.wait_ge(rope_done, it * PROJ + (u_of(s)[-1] + 1))
                        pe.wait_ge(masked_done, tick0 + s)
                        for b in range(GB):
                            last = nc.tensor.matmul(score_ps[:, b * S:(b + 1) * S], q_rot[:, b].rearrange("p h q -> p (h q)"),
                                                    k_rot[:, grp * GROUP + b * S:grp * GROUP + (b + 1) * S],
                                                    start=True, stop=True)
                        last.then_inc(scores_done, 1)
                        if s < TICKS - 1:
                            project_queries(s + 1)
                        if s >= 1:
                            if s == 1:
                                pe.wait_ge(v_copied, it * 2 + 2)
                            project_output(s - 1)
                        pe.wait_ge(probs_done, tick0 + (s + 1))
                        pe.wait_ge(probs_copied, tick0 + s)
                        pv = prob[:, :, :].rearrange("p b k -> p (b k)")
                        for t in range(GT):
                            last = nc.tensor.transpose(prob_ps[:, t * P:(t + 1) * P], pv[:, t * P:(t + 1) * P], eye[:, :])
                        last.then_inc(probs_turned, 1)
                        pe.wait_ge(probs_copied, tick0 + (s + 1))
                        pe.wait_ge(v_copied, it * 2 + 2)
                        pe.wait_ge(o_hi_ready, (tick0 + s) * 2)
                        pe.wait_ge(o_lo_ready, (tick0 + s) * 2)
                        for t in range(GT):
                            for b in range(2):
                                rows = slice(b * S, (b + 1) * S)
                                last = nc.tensor.matmul(attn_ps[b][:, t * P:(t + 1) * P], v_tok[rows, grp * GT + t, :],
                                                        prob_t[rows, t * P:(t + 1) * P], start=True, stop=True)
                        last.then_inc(attn_done, 1)
                    project_output(TICKS - 1)
            pe.wait_ge(swap_done, NIT * PROJ)
            pe.wait_ge(cos_done, NIT * PROJ)
            with pe.Fori(0, HALVES) as half:
                pe.wait_ge(z_gated, half * TILES)
                turn_tokens(half + HALVES)
                pe.wait_ge(x_hi_ready, (half + HALVES) * TILES + TILES)
                pe.wait_ge(x_lo_ready, (half + HALVES) * TILES + TILES)
                pe.wait_ge(ffn_hi_ready, 3)
                pe.wait_ge(ffn_lo_ready, 3)
                pe.wait_ge(o_lo_ready, NIT * TICKS * 2)
                pe.wait_ge(route_copied, half * GROUPS)
                for j in range(GROUPS):
                    cols = slice(j * GROUP, (j + 1) * GROUP)
                    three_products(attn_ps[j][:, :], [
                        (router_hi[:, c, :], router_lo[:, c, :], x_hi[:, c, cols], x_lo[:, c, cols])
                        for c in range(EC)]).then_inc(route_done, 1)
                pe.wait_ge(route_copied, half * GROUPS + GROUPS)
                pe.wait_ge(logits_copied, half)
                pe.wait_ge(masked_done, NIT * TICKS)
                for t in range(TILES):
                    last = nc.tensor.matmul(score_ps[:, t * EXPERTS:(t + 1) * EXPERTS], route[:, t * P:(t + 1) * P],
                                            keys_sb[:, :], start=True, stop=True)
                last.then_inc(logits_done, 1)

                def bottleneck(t):
                    if t >= 2:
                        pe.wait_ge(z_gated, half * TILES + (t - 1))
                    tok = slice(t * P, (t + 1) * P)
                    three_products(proj_ps[t % 2][:, :], [
                        (x_hi[:, c, tok], x_lo[:, c, tok], a_hi[:, c, :], a_lo[:, c, :])
                        for c in range(EC)]).then_inc(z_done, 1)

                bottleneck(0)
                pe.wait_ge(y_added, NIT * YT)
                pe.wait_ge(probs_copied, NIT * TICKS)
                for t in range(TILES):
                    if t + 1 < TILES:
                        bottleneck(t + 1)
                    pe.wait_ge(z_gated, half * TILES + (t + 1))
                    pe.wait_ge(z_lo_ready, half * TILES + t)
                    for c in range(EC):
                        last = nc.tensor.transpose(prob_ps[:, c * P:(c + 1) * P],
                                                   straight[:, t % 2, c * P:(c + 1) * P], eye[:, :])
                    last.then_inc(z_turned, 1)
                    pe.wait_ge(z_hi_ready, half * TILES + (t + 1))
                    pe.wait_ge(z_lo_ready, half * TILES + (t + 1))
                    pe.wait_ge(final_done, half * TILES + max(t - 1, 0))
                    three_products(y_ps[t % 2][:, :], [
                        (o_hi[:, t % 2, c * P:(c + 1) * P], o_lo[:, t % 2, c * P:(c + 1) * P], b_hi[:, c, :], b_lo[:, c, :])
                        for c in range(EC)]).then_inc(ffn_done, 1)


def kernel(x, ctx_4096, pos_BxS2, mask_BxSxS2_ik0, g_xattn, g_ffn, L0_xattn_Wq, L0_xattn_Wk, L0_xattn_Wv,
           L0_xattn_Wo, L0_ffn_A_w, L0_ffn_B_w, L0_ffn_Wq_w, L0_ffn_keys):
    import numpy as np
    import concourse.bacc as bacc
    from concourse.bass_utils import run_bass_kernel_spmd

    def tiles(a):
        return a.reshape(T // P, P, a.shape[-1]).transpose(1, 0, 2)

    def chunks(a):
        return a.reshape(a.shape[0] // P, P, a.shape[1]).transpose(1, 0, 2)

    def stationary(w, cols):
        return w.reshape(EC, P, w.shape[1] // cols, cols).transpose(2, 1, 0, 3)

    inv_freq = (1.0 / np.float32(10000.0) ** (np.arange(0, D, 2, dtype=np.float32) / np.float32(D))).astype(np.float32)
    angle = np.arange(MAX_POS, dtype=np.float32)[:, None] * inv_freq[None, :]
    cos, sin = np.cos(angle), np.sin(angle)
    rope = np.concatenate([cos, cos, -sin, sin], axis=1).astype(np.float32)

    wk, wv = stationary(L0_xattn_Wk, D), stationary(L0_xattn_Wv, D)
    router = np.zeros((P, EC, P), L0_ffn_Wq_w.dtype)
    router[:, :, 0:ROUTER] = chunks(L0_ffn_Wq_w.T)
    arrays = {
        "x": tiles(x.reshape(T, E)),
        "ctx_t": ctx_4096.reshape(T, E).T,
        "mask": mask_BxSxS2_ik0.transpose(1, 0, 2).reshape(S, B * S),
        "pos": pos_BxS2.reshape(T // P, P).T,
        "gains": np.broadcast_to(np.concatenate([g_xattn, g_ffn]), (P, 2)),
        "wq": stationary(L0_xattn_Wq, 2 * D).reshape(KVH * PAIRS * P, EC * 2 * D),
        "wo": L0_xattn_Wo.reshape(KVH * PAIRS, 2, D, E).transpose(0, 2, 1, 3).reshape(KVH * PAIRS * P, 2 * E),
        "wkv": np.stack([wk, wv], axis=2).reshape(KVH * P, 2 * EC * D),
        "a_t": chunks(L0_ffn_A_w.T),
        "b_t": chunks(L0_ffn_B_w.T),
        "router_t": router,
        "keys_t": L0_ffn_keys.T,
        "rope": rope,
        "ident": np.eye(P, dtype=np.float32),
    }
    nc = bacc.Bacc("TRN2", target_bir_lowering=False, num_devices=1)
    arrays = {f"{n}_dram": np.ascontiguousarray(a) for n, a in arrays.items()}
    args = [nc.dram_tensor(n, a.shape, mybir.dt.from_np(a.dtype), kind="ExternalInput").ap() for n, a in arrays.items()]
    args.append(nc.dram_tensor("out_dram", (P, T // P, E), F32, kind="ExternalOutput").ap())
    flamingo_block(nc, *args)
    result = run_bass_kernel_spmd(nc, [arrays], core_ids=[0]).results[0]["out_dram"]
    return np.ascontiguousarray(result.transpose(1, 0, 2)).reshape(B, S, E)
```

```python
from contextlib import ExitStack

import concourse.bass as bass
from concourse import mybir

F32 = mybir.dt.float32
F32R = mybir.dt.float32r
BF16 = mybir.dt.bfloat16
I32 = mybir.dt.int32
U32 = mybir.dt.uint32
ALU = mybir.AluOpType
ACT = mybir.ActivationFunctionType
AX_X = mybir.AxisListType.X

P = 128
B, S, E = 32, 64, 512
H, KVH, D = 32, 8, 128
T = B * S
HALVES = 2
HT = T // HALVES
TILES = HT // P
HB = B // HALVES
EC = E // P
GROUP = 512
GROUPS = HT // GROUP
GT = GROUP // P
GB = GROUP // S
PAIRS = H // KVH // 2
TICKS = PAIRS * GROUPS
EXPERTS, RANK, TOP_K, ROUTER = 64, 8, 16, 16
N_B = EXPERTS * RANK
FFN_SCALE = 32 / TOP_K
MAX_POS = 512
MASKED = -1.0e30
REMOVED = -3.0e38
EPS = 1e-5
SM_SCALE = 1.0 / float(D) ** 0.5

SEQ = ["K0", "K1", "V0", "Q0a", "Q0b", "Q1a", "Q1b", "V1", "Q2a", "Q2b", "Q3a", "Q3b"]
PROJ = len(SEQ)
ROTATED = [name for name in SEQ if name[0] != "V"]
ROT = len(ROTATED)
YT = TICKS * GT
NIT = HALVES * KVH
POS_STEPS = 4
MOMENT_STEPS = 6
TRIG_COPIES = 2 * TILES // 4
GATE_STEPS = 6


def projection(name):
    return SEQ.index(name), ROTATED.index(name) if name in ROTATED else None, int(name[1]) % GROUPS


def queries(s):
    return [f"Q{s}a", f"Q{s}b"]


def turned_tiles(s):
    return 3 if s == TICKS - 1 else 2


def flamingo_block(nc, x, ctx_t, mask, pos, gains, wq, wo, wkv, a_t, b_t, router_t, keys_t, rope, ident, out):
    with ExitStack() as stack:
        def sb(name, shape, dt=F32):
            return stack.enter_context(nc.sbuf_tensor(name, shape, dt))

        def bank(name):
            return stack.enter_context(nc.psum_tensor(name, [P, 512], F32))

        def sem(name):
            return stack.enter_context(nc.semaphore(name))

        x_hi = sb("x_hi", [P, EC, HT], F32R)
        x_lo = sb("x_lo", [P, EC, HT], F32R)
        c_hi = sb("c_hi", [P, EC, HT], F32R)
        c_lo = sb("c_lo", [P, EC, HT], F32R)
        resid = sb("resid", [P, HALVES * TILES, E])
        mask_bias = sb("mask_bias", [P, HB, S], BF16)
        cos_t = sb("cos_t", [P, HT])
        sin_t = sb("sin_t", [P, HT])
        wq_hi = sb("wq_hi", [P, PAIRS, EC, 2 * D], F32R)
        wq_lo = sb("wq_lo", [P, PAIRS, EC, 2 * D], F32R)
        wo_hi = sb("wo_hi", [P, PAIRS, 2, E], F32R)
        wo_lo = sb("wo_lo", [P, PAIRS, 2, E], F32R)
        wkv_hi = sb("wkv_hi", [P, 2, EC, D], F32R)
        wkv_lo = sb("wkv_lo", [P, 2, EC, D], F32R)
        wq_raw = sb("wq_raw", [P, PAIRS, EC * 2 * D])
        wo_raw = sb("wo_raw", [P, PAIRS, 2 * E])
        wkv_raw = sb("wkv_raw", [P, 2 * EC * D])
        k_rot = sb("k_rot", [P, HT])
        v_tok = sb("v_tok", [P, TILES, D])
        swapped = sb("swapped", [P, 2, GROUP])
        straight = sb("straight", [P, 2, GROUP])
        q_rot = sb("q_rot", [P, GB, 2, S])
        score = sb("score", [P, GB, S])
        expo = sb("expo", [P, GB, S])
        prob = sb("prob", [P, GB, S])
        prob_t = sb("prob_t", [P, 512])
        o_hi = sb("o_hi", [P, 2, GROUP], F32R)
        o_lo = sb("o_lo", [P, 2, GROUP], F32R)
        eye = sb("eye", [P, P])
        row_max = sb("row_max", [P, GB])
        row_sum = sb("row_sum", [P, GB])
        row_inv = sb("row_inv", [P, GB])
        stats = sb("stats", [P, TILES, 6])
        mean = sb("mean", [P, TILES])
        gap = sb("gap", [P, TILES])
        var_eps = sb("var_eps", [P, TILES])
        minus_half = sb("minus_half", [P, TILES])
        rstd = sb("rstd", [P, TILES])
        gain = sb("gain", [P, 2])
        gate_gain = sb("gate_gain", [P, 3])
        pos_i = sb("pos_i", [P, TILES], I32)
        pos_f = sb("pos_f", [P, TILES])
        pos_w = sb("pos_w", [P, TILES])
        pos_u = sb("pos_u", [P, TILES], U32)
        keys_sb = sb("keys_sb", [ROUTER, EXPERTS])
        top_a = sb("top_a", [P, TILES, 8])
        top_b = sb("top_b", [P, TILES, 8])

        proj_ps = [bank("proj_ps0"), bank("proj_ps1")]
        score_ps = bank("score_ps")
        prob_ps = bank("prob_ps")
        attn_ps = [bank("attn_ps0"), bank("attn_ps1")]
        y_ps = [bank("y_ps0"), bank("y_ps1")]

        x_landed = [sem("x_landed0"), sem("x_landed1")]
        ctx_landed = [sem("ctx_landed0"), sem("ctx_landed1")]
        mask_landed = sem("mask_landed")
        pos_landed = sem("pos_landed")
        small_landed = sem("small_landed")
        wkv_landed = sem("wkv_landed")
        wq_landed = [sem("wq_landed0"), sem("wq_landed1")]
        wo_landed = [sem("wo_landed0"), sem("wo_landed1")]
        rope_landed = [sem(f"rope_landed{i}") for i in range(4)]
        a_landed = sem("a_landed")
        b_landed = sem("b_landed")
        router_landed = sem("router_landed")
        out_stored = [sem("out_stored0"), sem("out_stored1")]
        waits_passed = sem("waits_passed")
        wkv_hi_ready = sem("wkv_hi_ready")
        wkv_lo_ready = sem("wkv_lo_ready")
        wq_hi_ready = [sem("wq_hi_ready0"), sem("wq_hi_ready1")]
        wq_lo_ready = [sem("wq_lo_ready0"), sem("wq_lo_ready1")]
        wo_hi_ready = [sem("wo_hi_ready0"), sem("wo_hi_ready1")]
        wo_lo_ready = [sem("wo_lo_ready0"), sem("wo_lo_ready1")]
        ctx_hi_ready = sem("ctx_hi_ready")
        ctx_lo_ready = sem("ctx_lo_ready")
        ffn_hi_ready = sem("ffn_hi_ready")
        ffn_lo_ready = sem("ffn_lo_ready")
        stats_ready = sem("stats_ready")
        moment_step = sem("moment_step")
        var_ready = sem("var_ready")
        rstd_ready = sem("rstd_ready")
        half_ready = sem("half_ready")
        normed = sem("normed")
        x_turned = sem("x_turned")
        x_hi_ready = sem("x_hi_ready")
        x_lo_ready = sem("x_lo_ready")
        tanh_ready = sem("tanh_ready")
        gain_ready = sem("gain_ready")
        pos_step = sem("pos_step")
        trig_turned = sem("trig_turned")
        trig_ready = sem("trig_ready")
        bias_ready = sem("bias_ready")
        proj_done = sem("proj_done")
        swap_done = sem("swap_done")
        cos_done = sem("cos_done")
        sin_done = sem("sin_done")
        rope_done = sem("rope_done")
        v_turned = sem("v_turned")
        v_copied = sem("v_copied")
        scores_done = sem("scores_done")
        masked_done = sem("masked_done")
        max_done = sem("max_done")
        shift_done = sem("shift_done")
        exp_done = sem("exp_done")
        sum_done = sem("sum_done")
        inv_done = sem("inv_done")
        probs_done = sem("probs_done")
        probs_turned = sem("probs_turned")
        probs_copied = sem("probs_copied")
        attn_done = sem("attn_done")
        o_hi_ready = sem("o_hi_ready")
        o_lo_ready = sem("o_lo_ready")
        y_done = sem("y_done")
        y_added = sem("y_added")
        route_done = sem("route_done")
        route_copied = sem("route_copied")
        logits_done = sem("logits_done")
        logits_copied = sem("logits_copied")
        topk_step = sem("topk_step")
        gate_exp = sem("gate_exp")
        gate_step = sem("gate_step")
        z_done = sem("z_done")
        z_gated = sem("z_gated")
        z_turned = sem("z_turned")
        z_hi_ready = sem("z_hi_ready")
        z_lo_ready = sem("z_lo_ready")
        ffn_done = sem("ffn_done")
        final_done = sem("final_done")

        ctx_raw = [k_rot[:, :], v_tok[:, :, :].rearrange("p t d -> p (t d)")]
        mask_raw = q_rot[:, :, :, :].rearrange("p b h q -> p (b h q)").bitcast(I32)
        trig_rows = straight[:, :, :].rearrange("p s (u w) -> p (s u) w", w=2 * D)
        prob_t_v = prob_t[:, :]
        attn_v = [a[:, :].rearrange("p (t h q) -> p t h q", t=GT, h=2) for a in attn_ps]
        o_hi_v = o_hi[:, :, :].rearrange("p h (t b q) -> p b t h q", t=GT, b=2)
        o_lo_v = o_lo[:, :, :].rearrange("p h (t b q) -> p b t h q", t=GT, b=2)
        prob_v = prob[:, :, :].rearrange("p b k -> p (b k)")
        score_v = score[:, :, :].rearrange("p b k -> p (b k)")
        a_hi, a_lo = c_hi[:, :, 0:N_B], c_lo[:, :, 0:N_B]
        b_hi, b_lo = c_hi[:, :, N_B:N_B + E], c_lo[:, :, N_B:N_B + E]
        a_raw = wq_raw[:, :, :].rearrange("p a (c n) -> p (a c) n", n=N_B)
        b_raw = wo_raw[:, :, :].rearrange("p a (c n) -> p (a c) n", n=E)
        router_raw = wkv_raw[:, 0:EC * P].rearrange("p (c n) -> p c n", c=EC)
        router_hi, router_lo = wkv_hi[:, 0, :, :], wkv_lo[:, 0, :, :]
        route = k_rot[0:ROUTER, :]
        logits, struck, weight, gate = score, expo, prob, prob_t[:, :].rearrange("p (t e) -> p t e", e=EXPERTS)
        tile_out = q_rot[:, :, :, :].rearrange("p (s b) h q -> p s (b h q)", s=2)

        ffn_splits = [(router_lo, router_raw, router_hi), (a_lo, a_raw, a_hi), (b_lo, b_raw, b_hi)]

        def flat(w):
            return w[:, :, :, :].rearrange("p k c n -> p (k c n)")

        def per_row(ap, n):
            return ap.unsqueeze(2).to_broadcast([P, ap.shape[1], n])

        def wait_alone(engine, semaphore, value):
            engine.wait_ge(semaphore, value)
            engine.sem_inc(waits_passed, 1)

        block = stack.enter_context(nc.Block())

        def row_of(buffer, half, t):
            return buffer[:, bass.ds(half * TILES + t, 1), :].rearrange("p a e -> p (a e)")

        def flat3(w):
            return w.rearrange("p c n -> p (c n)")

        @block.sync
        def _(sp):
            with sp.Fori(0, HALVES) as half:
                tile0, token0, mask0 = sp.snap(half * TILES), sp.snap(half * HT), sp.snap(half * (HB * S))
                wait_alone(sp, pos_step, half * POS_STEPS)
                sp.dma_start(pos_i[:, :], pos[:, bass.ds(tile0, TILES)]).then_inc(pos_landed, 16)
                sp.wait_ge(scores_done, half * (KVH * TICKS))
                sp.wait_ge(attn_done, half * (KVH * TICKS))
                for c in range(EC):
                    if c >= 2:
                        sp.wait_ge(ctx_hi_ready, half * EC + (c - 1))
                        sp.wait_ge(ctx_lo_ready, half * EC + (c - 1))
                    sp.dma_start(ctx_raw[c % 2],
                                 ctx_t[c * P:(c + 1) * P, bass.ds(token0, HT)]).then_inc(ctx_landed[c % 2], 16)
                for r in range(2):
                    sp.dma_start(mask_raw[r * S:(r + 1) * S, :],
                                 mask[:, bass.ds(mask0, HB * S)]).then_inc(mask_landed, 16)
                with sp.Fori(0, KVH) as g:
                    it = half * KVH + g
                    pair_row = [sp.snap((g * PAIRS + pair) * P) for pair in range(PAIRS)]
                    g_next = (g + 1) % KVH
                    wkv_row, wq_row = sp.snap(g_next * P), sp.snap(g_next * (PAIRS * P))
                    sp.wait_ge(wq_hi_ready[1], it)
                    sp.wait_ge(wq_lo_ready[1], it)
                    sp.dma_start(wq_raw[:, 1, :], wq[bass.ds(pair_row[1], P), :]).then_inc(wq_landed[1], 16)
                    for pair in range(PAIRS):
                        sp.wait_ge(wo_hi_ready[pair], it)
                        sp.wait_ge(wo_lo_ready[pair], it)
                        sp.dma_start(wo_raw[:, pair, :],
                                     wo[bass.ds(pair_row[pair], P), :]).then_inc(wo_landed[pair], 16)
                    sp.wait_ge(wkv_hi_ready, it + 1)
                    sp.wait_ge(wkv_lo_ready, it + 1)
                    sp.dma_start(wkv_raw[:, :], wkv[bass.ds(wkv_row, P), :]).then_inc(wkv_landed, 16)
                    sp.wait_ge(wq_hi_ready[0], it + 1)
                    sp.wait_ge(wq_lo_ready[0], it + 1)
                    sp.dma_start(wq_raw[:, 0, :], wq[bass.ds(wq_row, P), :]).then_inc(wq_landed[0], 16)
            for pair in range(PAIRS):
                sp.wait_ge(wq_hi_ready[pair], NIT + 1 - pair)
                sp.wait_ge(wq_lo_ready[pair], NIT + 1 - pair)
                sp.wait_ge(wo_hi_ready[pair], NIT)
                sp.wait_ge(wo_lo_ready[pair], NIT)
            sp.wait_ge(wkv_hi_ready, NIT + 1)
            sp.wait_ge(wkv_lo_ready, NIT + 1)
            sp.dma_start(router_raw, router_t).then_inc(router_landed, 16)
            sp.dma_start(a_raw, a_t).then_inc(a_landed, 16)
            sp.dma_start(b_raw, b_t).then_inc(b_landed, 16)
            with sp.Fori(0, HALVES) as half:
                for t in range(TILES):
                    tile = sp.snap(half * TILES + t)
                    sp.wait_ge(final_done, half * TILES + t + 1)
                    sp.dma_start(out[:, bass.ds(tile, 1), :],
                                 tile_out[:, t % 2:t % 2 + 1, :]).then_inc(out_stored[t % 2], 16)
            for s in out_stored:
                sp.wait_ge(s, 16 * (HALVES * TILES // 2))

        @block.gpsimd
        def _(pool):
            def weights_lo(lo, raw, hi, hi_ready, lo_ready, n):
                pool.wait_ge(hi_ready, n)
                nc.gpsimd.tensor_tensor(lo, raw, hi.bitcast(F32), ALU.subtract).then_inc(lo_ready, 1)

            def wkv_part(n):
                weights_lo(flat(wkv_lo), wkv_raw[:, :], flat(wkv_hi), wkv_hi_ready, wkv_lo_ready, n)

            def wq_part(pair, n):
                weights_lo(flat3(wq_lo[:, pair]), wq_raw[:, pair, :], flat3(wq_hi[:, pair]),
                           wq_hi_ready[pair], wq_lo_ready[pair], n)

            def wo_part(pair, n):
                weights_lo(flat3(wo_lo[:, pair]), wo_raw[:, pair, :], flat3(wo_hi[:, pair]),
                           wo_hi_ready[pair], wo_lo_ready[pair], n)

            def gather(half, t):
                if t >= 4:
                    wait_alone(pool, trig_turned, half * TILES + (t - 3))
                pool.indirect_dma_start(out=trig_rows[:, t % 4, :], out_offset=None, in_=rope,
                                        in_offset=bass.IndirectOffsetOnAxis(ap=pos_u[:, t:t + 1], axis=0)
                                        ).then_inc(rope_landed[t % 4], 16)

            def inverse_root(n):
                pool.wait_ge(var_ready, n + 1)
                nc.gpsimd.tensor_tensor(rstd[:, :], var_eps[:, :], minus_half[:, :], ALU.pow).then_inc(rstd_ready, 1)

            def iteration(half, it, first):
                def times_sin(name):
                    u, r, grp = projection(name)
                    pool.wait_ge(swap_done, it * PROJ + (u + 1))
                    nc.gpsimd.tensor_tensor(swapped[:, u % 2, :], swapped[:, u % 2, :],
                                            sin_t[:, grp * GROUP:(grp + 1) * GROUP], ALU.mult).then_inc(sin_done, 1)

                if first:
                    inverse_root(half)
                times_sin("K0")
                times_sin("K1")
                times_sin("Q0a")
                wq_part(1, it + 1)
                times_sin("Q0b")
                wo_part(0, it + 1)
                for s in range(TICKS):
                    if s < TICKS - 1:
                        for name in queries(s + 1):
                            times_sin(name)
                    if s == 0:
                        wo_part(1, it + 1)
                    if s == 2:
                        wkv_part(it + 2)
                    if s == 3:
                        wq_part(0, it + 2)

            nc.gpsimd.memset(minus_half[:, :], -0.5).then_inc(half_ready, 1)
            pool.wait_ge(half_ready, 1)
            with pool.Fori(0, HALVES) as half:
                pool.wait_ge(rope_done, half * (KVH * ROT))
                wait_alone(pool, pos_step, half * POS_STEPS + POS_STEPS)
                for t in range(TILES):
                    gather(half, t)
                pool.wait_ge(trig_ready, half * TRIG_COPIES + TRIG_COPIES)
                iteration(half, half * KVH, True)
                with pool.Fori(1, KVH) as g:
                    iteration(half, half * KVH + g, False)
            for n, (lo, raw, hi) in enumerate(ffn_splits):
                pool.wait_ge(ffn_hi_ready, n + 1)
                nc.gpsimd.tensor_tensor(lo, raw, hi.bitcast(F32), ALU.subtract).then_inc(ffn_lo_ready, 1)
            with pool.Fori(0, HALVES) as half:
                inverse_root(half + HALVES)

        @block.scalar
        def _(act):
            def weights_hi(hi, raw, landed, ready, n):
                act.wait_ge(landed, 16 * n)
                nc.scalar.copy(hi, raw).then_inc(ready, 1)

            def wkv_part(n):
                weights_hi(flat(wkv_hi), wkv_raw[:, :], wkv_landed, wkv_hi_ready, n)

            def wq_part(pair, n):
                weights_hi(flat3(wq_hi[:, pair]), wq_raw[:, pair, :], wq_landed[pair], wq_hi_ready[pair], n)

            def wo_part(pair, n):
                weights_hi(flat3(wo_hi[:, pair]), wo_raw[:, pair, :], wo_landed[pair], wo_hi_ready[pair], n)

            def turned_hi(n0, t):
                act.wait_ge(x_turned, n0 + (t + 1))
                nc.scalar.copy(x_hi[:, :, t * P:(t + 1) * P],
                               proj_ps[t % 2][:, :].rearrange("p (c n) -> p c n", c=EC)).then_inc(x_hi_ready, 1)

            def iteration(half, it, first):
                tick0 = it * TICKS

                def staging_free(u):
                    if u < 2:
                        act.wait_ge(rope_done, it * ROT)
                    else:
                        _, r, _ = projection(SEQ[u - 2])
                        if r is None:
                            act.wait_ge(v_turned, it * GROUPS + (int(SEQ[u - 2][1]) + 1))
                        else:
                            act.wait_ge(rope_done, it * ROT + (r + 1))

                def swap(name):
                    u, r, _ = projection(name)
                    act.wait_ge(proj_done, it * PROJ + (u + 1))
                    staging_free(u)
                    ps = proj_ps[u % 2]
                    nc.scalar.copy(swapped[0:D // 2, u % 2, :], ps[D // 2:D, :])
                    nc.scalar.copy(swapped[D // 2:D, u % 2, :], ps[0:D // 2, :]).then_inc(swap_done, 1)

                def copy_values(name):
                    u, _, _ = projection(name)
                    act.wait_ge(proj_done, it * PROJ + (u + 1))
                    staging_free(u)
                    nc.scalar.copy(swapped[:, u % 2, :], proj_ps[u % 2][:, :]).then_inc(swap_done, 1)

                swap("K0")
                swap("K1")
                copy_values("V0")
                if first:
                    for t in range(TILES):
                        turned_hi(half * TILES, t)
                wq_part(1, it + 1)
                swap("Q0a")
                swap("Q0b")
                act.wait_ge(y_done, it * YT if first else it * YT - YT // 2)
                wo_part(0, it + 1)
                for s in range(TICKS):
                    act.wait_ge(shift_done, tick0 + (s + 1))
                    act.wait_ge(probs_done, tick0 + s)
                    nc.scalar.activation(expo[:, :, :], score[:, :, :], ACT.Exp, scale=SM_SCALE).then_inc(exp_done, 1)
                    if s < TICKS - 1:
                        for name in queries(s + 1):
                            swap(name)
                    if s == 2:
                        wkv_part(it + 2)
                    if s == 3:
                        wq_part(0, it + 2)
                    act.wait_ge(probs_turned, tick0 + (s + 1))
                    act.wait_ge(attn_done, tick0 + s)
                    nc.scalar.copy(prob_t[:, :], prob_ps[:, :]).then_inc(probs_copied, 1)
                    if s == 0:
                        copy_values("V1")
                    act.wait_ge(attn_done, tick0 + (s + 1))
                    act.wait_ge(y_done, (tick0 + s) * GT)
                    for b in range(2):
                        nc.scalar.copy(o_hi_v[:, b], attn_v[b]).then_inc(o_hi_ready, 1)
                    if s == 0:
                        wo_part(1, it + 1)

            act.dma_start(wkv_raw[:, :], wkv[0:P, :]).then_inc(wkv_landed, 16)
            act.dma_start(eye[:, :], ident).then_inc(small_landed, 16)
            act.dma_start(gain[:, :], gains).then_inc(small_landed, 16)
            act.dma_start(keys_sb[:, :], keys_t).then_inc(small_landed, 16)
            act.dma_start(wq_raw[:, 0, :], wq[0:P, :]).then_inc(wq_landed[0], 16)
            for i in range(2):
                act.dma_start(resid[:, i * TILES:(i + 1) * TILES, :],
                              x[:, i * TILES:(i + 1) * TILES, :]).then_inc(x_landed[i], 16)
            act.wait_ge(small_landed, 48)
            nc.scalar.activation(gate_gain[:, 0:2], gain[:, :], ACT.Tanh).then_inc(tanh_ready, 1)
            wkv_part(1)
            wq_part(0, 1)
            with act.Fori(0, HALVES) as half:
                for c in range(EC):
                    act.wait_ge(ctx_landed[c % 2], half * (16 * EC // 2) + 16 * (c // 2 + 1))
                    if c == 0:
                        act.wait_ge(proj_done, half * (PROJ * KVH))
                    nc.scalar.copy(c_hi[:, c, :], ctx_raw[c % 2]).then_inc(ctx_hi_ready, 1)
                act.wait_ge(cos_done, half * (ROT * KVH))
                act.wait_ge(sin_done, half * (ROT * KVH))
                for r in range(TILES // 4):
                    act.wait_ge(trig_turned, half * TILES + 4 * (r + 1))
                    nc.scalar.copy(cos_t[:, r * 512:(r + 1) * 512], score_ps[:, :]).then_inc(trig_ready, 1)
                    nc.scalar.copy(sin_t[:, r * 512:(r + 1) * 512], prob_ps[:, :]).then_inc(trig_ready, 1)
                iteration(half, half * KVH, True)
                with act.Fori(1, KVH) as g:
                    iteration(half, half * KVH + g, False)
            act.wait_ge(proj_done, NIT * PROJ)
            for n, (lo, raw, hi) in enumerate(ffn_splits):
                act.wait_ge([router_landed, a_landed, b_landed][n], 16)
                nc.scalar.copy(hi, raw).then_inc(ffn_hi_ready, 1)
            with act.Fori(0, HALVES) as half:
                act.wait_ge(z_done, half * TILES)
                for t in range(TILES):
                    turned_hi(half * TILES + HALVES * TILES, t)
                act.wait_ge(logits_done, half)
                for c in range(GROUPS):
                    act.wait_ge(route_done, half * GROUPS + (c + 1))
                    nc.scalar.copy(route[:, c * GROUP:(c + 1) * GROUP],
                                   attn_ps[c][0:ROUTER, :]).then_inc(route_copied, 1)
                act.wait_ge(gate_step, half * GATE_STEPS + 1)
                nc.scalar.activation(weight[:, :, :], weight[:, :, :], ACT.Exp).then_inc(gate_exp, 1)
                for t in range(TILES):
                    act.wait_ge(z_turned, half * TILES + (t + 1))
                    if t >= 2:
                        act.wait_ge(ffn_done, half * TILES + (t - 1))
                    else:
                        act.wait_ge(ffn_done, half * TILES)
                    nc.scalar.copy(o_hi[:, t % 2, :], prob_ps[:, :]).then_inc(z_hi_ready, 1)

        @block.vector
        def _(dve):
            def token_stats(half, n):
                for t in range(TILES):
                    nc.vector.bn_stats(stats[:, t, :], row_of(resid, half, t)).then_inc(stats_ready, 1)
                mean_a, mean_b = stats[:, :, 1], stats[:, :, 4]
                dve.wait_ge(stats_ready, n * TILES + TILES)
                nc.vector.tensor_tensor(mean[:, :], mean_a, mean_b, ALU.add).then_inc(moment_step, 1)
                nc.vector.tensor_tensor(gap[:, :], mean_a, mean_b, ALU.subtract).then_inc(moment_step, 1)
                nc.vector.tensor_tensor(var_eps[:, :], stats[:, :, 2], stats[:, :, 5], ALU.add).then_inc(moment_step, 1)
                dve.wait_ge(moment_step, n * MOMENT_STEPS + 3)
                nc.vector.tensor_scalar(mean[:, :], mean[:, :], 0.5, None, ALU.mult).then_inc(moment_step, 1)
                nc.vector.tensor_tensor(gap[:, :], gap[:, :], gap[:, :], ALU.mult).then_inc(moment_step, 1)
                nc.vector.tensor_scalar(var_eps[:, :], var_eps[:, :], 1.0 / E, EPS, ALU.mult, ALU.add).then_inc(moment_step, 1)
                dve.wait_ge(moment_step, n * MOMENT_STEPS + 6)
                nc.vector.scalar_tensor_tensor(out=var_eps[:, :], in0=gap[:, :], scalar=0.25, in1=var_eps[:, :],
                                               op0=ALU.mult, op1=ALU.add).then_inc(var_ready, 1)

            def normalise_tokens(half, n):
                dve.wait_ge(rstd_ready, n + 1)

                def normalise(t):
                    if t >= 2:
                        dve.wait_ge(x_turned, n * TILES + (t - 1))
                    nc.vector.tensor_scalar(swapped[:, t % 2, :], row_of(resid, half, t), mean[:, t:t + 1],
                                            rstd[:, t:t + 1], ALU.subtract, ALU.mult).then_inc(normed, 1)

                normalise(0)
                for t in range(TILES):
                    if t + 1 < TILES:
                        normalise(t + 1)
                    dve.wait_ge(x_hi_ready, n * TILES + (t + 1))
                    nc.vector.tensor_tensor(x_lo[:, :, t * P:(t + 1) * P],
                                            proj_ps[t % 2][:, :].rearrange("p (c n) -> p c n", c=EC),
                                            x_hi[:, :, t * P:(t + 1) * P].bitcast(F32),
                                            ALU.subtract).then_inc(x_lo_ready, 1)

            def iteration(half, it, first):
                tick0 = it * TICKS

                def times_cos(name):
                    u, r, grp = projection(name)
                    dve.wait_ge(swap_done, it * PROJ + (u + 1))
                    dve.wait_ge(rope_done, it * ROT + max(r - 1, 0))
                    nc.vector.tensor_tensor(straight[:, r % 2, :], proj_ps[u % 2][:, :],
                                            cos_t[:, grp * GROUP:(grp + 1) * GROUP], ALU.mult).then_inc(cos_done, 1)

                def add_rotated(name):
                    u, r, grp = projection(name)
                    dve.wait_ge(cos_done, it * ROT + (r + 1))
                    dve.wait_ge(sin_done, it * ROT + (r + 1))
                    if name[0] == "K":
                        dve.wait_ge(scores_done, tick0)
                        dst = k_rot[:, grp * GROUP:(grp + 1) * GROUP].rearrange("p (b q) -> p b q", q=S)
                    else:
                        dve.wait_ge(scores_done, tick0 + int(name[1]))
                        dst = q_rot[:, :, "ab".index(name[2]), :]
                    nc.vector.tensor_tensor(dst, straight[:, r % 2, :].rearrange("p (b q) -> p b q", q=S),
                                            swapped[:, u % 2, :].rearrange("p (b q) -> p b q", q=S),
                                            ALU.add).then_inc(rope_done, 1)

                def keep_values(j):
                    dve.wait_ge(v_turned, it * GROUPS + (j + 1))
                    dve.wait_ge(attn_done, tick0)
                    nc.vector.tensor_copy(v_tok[:, j * GT:(j + 1) * GT, :].rearrange("p t d -> p (t d)"),
                                          y_ps[j][:, :]).then_inc(v_copied, 1)

                def add_output(base, s, t):
                    n = base + (s * GT + t)
                    dve.wait_ge(y_done, n + 1)
                    dve.wait_ge(y_added, n - t)
                    r = row_of(resid, half, (s % GROUPS) * GT + t)
                    nc.vector.scalar_tensor_tensor(out=r, in0=y_ps[t % 2][:, :], scalar=gate_gain[:, 0:1],
                                                   in1=r, op0=ALU.mult, op1=ALU.add).then_inc(y_added, 1)

                times_cos("K0")
                add_rotated("K0")
                times_cos("K1")
                add_rotated("K1")
                if first:
                    keep_values(0)
                    dve.wait_ge(rope_done, it * ROT + 2)
                    normalise_tokens(half, half)
                times_cos("Q0a")
                add_rotated("Q0a")
                if not first:
                    keep_values(0)
                times_cos("Q0b")
                if not first:
                    add_output(it * YT - YT, TICKS - 1, 0)
                add_rotated("Q0b")
                if not first:
                    for t in range(1, GT):
                        add_output(it * YT - YT, TICKS - 1, t)
                for s in range(TICKS):
                    grp = s % GROUPS
                    bias = mask_bias[:, grp * GB:(grp + 1) * GB, :].rearrange("p b k -> p (b k)")
                    dve.wait_ge(scores_done, tick0 + (s + 1))
                    dve.wait_ge(exp_done, tick0 + s)
                    nc.vector.tensor_tensor(score_v, score_ps[:, :], bias, ALU.add).then_inc(masked_done, 1)
                    dve.wait_ge(masked_done, tick0 + (s + 1))
                    nc.vector.reduce_max(row_max[:, :], score[:, :, :], AX_X).then_inc(max_done, 1)
                    dve.wait_ge(max_done, tick0 + (s + 1))
                    nc.vector.tensor_tensor(score[:, :, :], score[:, :, :], per_row(row_max[:, :], S),
                                            ALU.subtract).then_inc(shift_done, 1)
                    if s < TICKS - 1:
                        times_cos(queries(s + 1)[0])
                    else:
                        add_output(it * YT, s - 1, 0)
                    dve.wait_ge(exp_done, tick0 + (s + 1))
                    nc.vector.reduce_sum(row_sum[:, :], expo[:, :, :], AX_X).then_inc(sum_done, 1)
                    dve.wait_ge(sum_done, tick0 + (s + 1))
                    nc.vector.reciprocal(row_inv[:, :], row_sum[:, :]).then_inc(inv_done, 1)
                    dve.wait_ge(inv_done, tick0 + (s + 1))
                    dve.wait_ge(probs_turned, tick0 + s)
                    nc.vector.tensor_tensor(prob[:, :, :], expo[:, :, :], per_row(row_inv[:, :], S),
                                            ALU.mult).then_inc(probs_done, 1)
                    if s < TICKS - 1:
                        add_rotated(queries(s + 1)[0])
                        times_cos(queries(s + 1)[1])
                        if s >= 1:
                            add_output(it * YT, s - 1, 0)
                            add_output(it * YT, s - 1, 1)
                        add_rotated(queries(s + 1)[1])
                        if s >= 1:
                            add_output(it * YT, s - 1, 2)
                            add_output(it * YT, s - 1, 3)
                    else:
                        for t in range(1, GT):
                            add_output(it * YT, s - 1, t)
                    dve.wait_ge(y_done, (tick0 + s) * GT)
                    for b in range(2):
                        dve.wait_ge(o_hi_ready, (tick0 + s) * 2 + (b + 1))
                        nc.vector.tensor_tensor(o_lo_v[:, b], attn_v[b], o_hi_v[:, b].bitcast(F32),
                                                ALU.subtract).then_inc(o_lo_ready, 1)
                    if s == 0:
                        keep_values(1)
                return add_output

            def first_lo(lo, raw, hi, hi_ready, lo_ready):
                dve.wait_ge(hi_ready, 1)
                nc.vector.tensor_tensor(lo, raw, hi.bitcast(F32), ALU.subtract).then_inc(lo_ready, 1)

            first_lo(flat(wkv_lo), wkv_raw[:, :], flat(wkv_hi), wkv_hi_ready, wkv_lo_ready)
            first_lo(flat3(wq_lo[:, 0]), wq_raw[:, 0, :], flat3(wq_hi[:, 0]), wq_hi_ready[0], wq_lo_ready[0])
            dve.wait_ge(tanh_ready, 1)
            nc.vector.tensor_scalar(gate_gain[:, 2:3], gate_gain[:, 1:2], FFN_SCALE, None, ALU.mult).then_inc(gain_ready, 1)
            with dve.Fori(0, HALVES) as half:
                dve.wait_ge(pos_landed, half * 16 + 16)
                step0 = half * POS_STEPS
                nc.vector.tensor_copy(pos_f[:, :], pos_i[:, :]).then_inc(pos_step, 1)
                dve.wait_ge(pos_step, step0 + 1)
                nc.vector.tensor_scalar(pos_w[:, :], pos_f[:, :], 0.0, float(MAX_POS), ALU.is_lt, ALU.mult).then_inc(pos_step, 1)
                dve.wait_ge(pos_step, step0 + 2)
                nc.vector.tensor_tensor(pos_f[:, :], pos_f[:, :], pos_w[:, :], ALU.add).then_inc(pos_step, 1)
                dve.wait_ge(pos_step, step0 + 3)
                for i in range(4):
                    dve.wait_ge(rope_landed[i], half * (16 * TILES // 4))
                nc.vector.tensor_scalar(pos_u[:, :], pos_f[:, :], 0.0, float(MAX_POS - 1), ALU.max, ALU.min).then_inc(pos_step, 1)
                dve.wait_ge(proj_done, half * (PROJ * KVH))
                for c in range(EC):
                    dve.wait_ge(ctx_hi_ready, half * EC + (c + 1))
                    nc.vector.tensor_tensor(c_lo[:, c, :], ctx_raw[c % 2], c_hi[:, c, :].bitcast(F32),
                                            ALU.subtract).then_inc(ctx_lo_ready, 1)
                for i in range(2):
                    dve.wait_ge(x_landed[i], 16)
                dve.wait_ge(normed, half * TILES)
                token_stats(half, half)
                dve.wait_ge(mask_landed, half * 32 + 32)
                dve.wait_ge(masked_done, half * (KVH * TICKS))
                nc.vector.tensor_scalar(mask_bias[:, :, :].rearrange("p b k -> p (b k)"), mask_raw, 0.0, MASKED,
                                        ALU.is_equal, ALU.mult).then_inc(bias_ready, 1)
                dve.wait_ge(bias_ready, half + 1)
                dve.wait_ge(trig_ready, half * TRIG_COPIES + TRIG_COPIES)
                iteration(half, half * KVH, True)
                with dve.Fori(1, KVH) as g:
                    add_output = iteration(half, half * KVH + g, False)
                for t in range(GT):
                    add_output((half + 1) * (KVH * YT) - YT, TICKS - 1, t)
            dve.wait_ge(y_added, NIT * YT)
            dve.wait_ge(rope_done, NIT * ROT)
            dve.wait_ge(gain_ready, 1)
            with dve.Fori(0, HALVES) as half:
                dve.wait_ge(z_done, half * TILES)
                token_stats(half, half + HALVES)
                normalise_tokens(half, half + HALVES)
                dve.wait_ge(logits_done, half + 1)
                dve.wait_ge(z_gated, half * TILES)
                nc.vector.tensor_copy(score_v, score_ps[:, :]).then_inc(logits_copied, 1)
                wait_alone(dve, logits_copied, half + 1)
                steps = half * (4 * TILES)
                for t in range(TILES):
                    nc.vector.max(top_a[:, t, :], logits[:, t, :]).then_inc(topk_step, 1)
                wait_alone(dve, topk_step, steps + TILES)
                for t in range(TILES):
                    nc.vector.match_replace(struck[:, t, :], top_a[:, t, :], logits[:, t, :], REMOVED).then_inc(topk_step, 1)
                wait_alone(dve, topk_step, steps + 2 * TILES)
                for t in range(TILES):
                    nc.vector.max(top_b[:, t, :], struck[:, t, :]).then_inc(topk_step, 1)
                wait_alone(dve, topk_step, steps + 3 * TILES)
                for t in range(TILES):
                    nc.vector.match_replace(struck[:, t, :], top_b[:, t, :], struck[:, t, :], REMOVED).then_inc(topk_step, 1)
                dve.wait_ge(topk_step, steps + 4 * TILES)
                gates0 = half * GATE_STEPS
                nc.vector.tensor_tensor(weight[:, :, :], logits[:, :, :], top_a[:, :, 0:1].to_broadcast([P, TILES, EXPERTS]),
                                        ALU.subtract).then_inc(gate_step, 1)
                dve.wait_ge(gate_step, gates0 + 1)
                nc.vector.tensor_tensor(struck[:, :, :], struck[:, :, :], logits[:, :, :], ALU.not_equal).then_inc(gate_step, 1)
                dve.wait_ge(gate_step, gates0 + 2)
                dve.wait_ge(gate_exp, half + 1)
                nc.vector.tensor_tensor(weight[:, :, :], weight[:, :, :], struck[:, :, :], ALU.mult).then_inc(gate_step, 1)
                dve.wait_ge(gate_step, gates0 + 3)
                nc.vector.reduce_sum(row_sum[:, :], weight[:, :, :], AX_X).then_inc(gate_step, 1)
                dve.wait_ge(gate_step, gates0 + 4)
                nc.vector.reciprocal(row_inv[:, :], row_sum[:, :]).then_inc(gate_step, 1)
                dve.wait_ge(gate_step, gates0 + 5)
                nc.vector.tensor_tensor(gate, weight[:, :, :], per_row(row_inv[:, :], EXPERTS), ALU.mult).then_inc(gate_step, 1)
                dve.wait_ge(gate_step, gates0 + 6)

                def gate_z(t):
                    dve.wait_ge(z_done, half * TILES + (t + 1))
                    dve.wait_ge(z_turned, half * TILES + max(t - 1, 0))
                    nc.vector.tensor_tensor(straight[:, t % 2, :].rearrange("p (e r) -> p e r", r=RANK),
                                            proj_ps[t % 2][:, :].rearrange("p (e r) -> p e r", r=RANK),
                                            per_row(gate[:, t, :], RANK), ALU.mult).then_inc(z_gated, 1)

                gate_z(0)
                for t in range(TILES):
                    if t + 1 < TILES:
                        gate_z(t + 1)
                    dve.wait_ge(z_hi_ready, half * TILES + (t + 1))
                    dve.wait_ge(ffn_done, half * TILES + max(t - 1, 0))
                    nc.vector.tensor_tensor(o_lo[:, t % 2, :], prob_ps[:, :], o_hi[:, t % 2, :].bitcast(F32),
                                            ALU.subtract).then_inc(z_lo_ready, 1)
                    dve.wait_ge(ffn_done, half * TILES + (t + 1))
                    dve.wait_ge(out_stored[t % 2], half * (8 * TILES) + 16 * (t // 2))
                    nc.vector.scalar_tensor_tensor(out=tile_out[:, t % 2, :], in0=y_ps[t % 2][:, :],
                                                   scalar=gate_gain[:, 2:3],
                                                   in1=resid[:, bass.ds(half * TILES + t, 1), :].rearrange("p a e -> p (a e)"),
                                                   op0=ALU.mult, op1=ALU.add).then_inc(final_done, 1)

        @block.tensor
        def _(pe):
            def turn_tokens(n):
                for t in range(TILES):
                    pe.wait_ge(normed, n * TILES + (t + 1))
                    if t >= 2:
                        pe.wait_ge(x_lo_ready, n * TILES + (t - 1))
                    for c in range(EC):
                        last = nc.tensor.transpose(proj_ps[t % 2][:, c * P:(c + 1) * P],
                                                   swapped[:, t % 2, c * P:(c + 1) * P], eye[:, :])
                    last.then_inc(x_turned, 1)

            def three_products(ps, parts):
                n = len(parts)
                for i, (l_hi, l_lo, r_hi, r_lo) in enumerate(parts):
                    nc.tensor.matmul(ps, l_hi, r_hi, start=(i == 0), stop=False)
                    nc.tensor.matmul(ps, l_hi, r_lo, start=False, stop=False)
                    last = nc.tensor.matmul(ps, l_lo, r_hi, start=False, stop=(i == n - 1))
                return last

            def iteration(half, it, first):
                tick0 = it * TICKS

                def bank_free(u):
                    if u < 2:
                        pe.wait_ge(cos_done, it * ROT)
                        return
                    _, r, _ = projection(SEQ[u - 2])
                    if r is None:
                        pe.wait_ge(swap_done, it * PROJ + (u - 1))
                    else:
                        pe.wait_ge(cos_done, it * ROT + (r + 1))

                def project_context(name):
                    u, _, grp = projection(name)
                    bank_free(u)
                    k = "KV".index(name[0])
                    cols = slice(grp * GROUP, (grp + 1) * GROUP)
                    three_products(proj_ps[u % 2][:, :], [
                        (wkv_hi[:, k, c, :], wkv_lo[:, k, c, :], c_hi[:, c, cols], c_lo[:, c, cols])
                        for c in range(EC)]).then_inc(proj_done, 1)

                def project_queries(s):
                    pair = s // GROUPS
                    pe.wait_ge(wq_hi_ready[pair], it + 1)
                    pe.wait_ge(wq_lo_ready[pair], it + 1)
                    for head, name in enumerate(queries(s)):
                        if name == "Q0b" and not first:
                            turn_values(0)
                        u, _, grp = projection(name)
                        cols = slice(grp * GROUP, (grp + 1) * GROUP)
                        bank_free(u)
                        d = slice(head * D, (head + 1) * D)
                        three_products(proj_ps[u % 2][:, :], [
                            (wq_hi[:, pair, c, d], wq_lo[:, pair, c, d], x_hi[:, c, cols], x_lo[:, c, cols])
                            for c in range(EC)]).then_inc(proj_done, 1)

                def turn_values(j):
                    u = SEQ.index(f"V{j}")
                    pe.wait_ge(swap_done, it * PROJ + (u + 1))
                    pe.wait_ge(y_added, it * YT if first or j == 1 else it * YT - GT)
                    for t in range(GT):
                        last = nc.tensor.transpose(y_ps[j][:, t * D:(t + 1) * D],
                                                   swapped[:, u % 2, t * P:(t + 1) * P], eye[:, :])
                    last.then_inc(v_turned, 1)

                def project_output(base, weights, s, tiles):
                    pair = s // GROUPS
                    pe.wait_ge(wo_hi_ready[pair], weights)
                    pe.wait_ge(wo_lo_ready[pair], weights)
                    for t in tiles:
                        n = base + (s * GT + t)
                        if s == 0 and t < 2:
                            pe.wait_ge(y_added, base)
                            pe.wait_ge(v_copied, it * GROUPS + (t + 1))
                        else:
                            pe.wait_ge(y_added, n - 1)
                        tok = slice(t * P, (t + 1) * P)
                        three_products(y_ps[t % 2][:, :], [
                            (o_hi[:, h, tok], o_lo[:, h, tok], wo_hi[:, pair, h, :], wo_lo[:, pair, h, :])
                            for h in range(2)]).then_inc(y_done, 1)

                def last_output(base, weights, attended):
                    pe.wait_ge(o_hi_ready, attended * 2)
                    pe.wait_ge(o_lo_ready, attended * 2)
                    project_output(base, weights, TICKS - 1, range(GT))

                if first:
                    pe.wait_ge(ctx_hi_ready, half * EC + EC)
                    pe.wait_ge(ctx_lo_ready, half * EC + EC)
                pe.wait_ge(wkv_hi_ready, it + 1)
                pe.wait_ge(wkv_lo_ready, it + 1)
                project_context("K0")
                project_context("K1")
                project_context("V0")
                if first:
                    turn_values(0)
                    pe.wait_ge(cos_done, it * ROT + 2)
                    turn_tokens(half)
                    pe.wait_ge(x_hi_ready, half * TILES + TILES)
                    pe.wait_ge(x_lo_ready, half * TILES + TILES)
                project_queries(0)
                if not first:
                    pe.wait_ge(v_copied, it * GROUPS + 1)
                    last_output(it * YT - YT, it, tick0)
                for s in range(TICKS):
                    grp = s % GROUPS
                    pe.wait_ge(rope_done, it * ROT + (ROTATED.index(queries(s)[1]) + 1))
                    pe.wait_ge(masked_done, tick0 + s)
                    for b in range(GB):
                        last = nc.tensor.matmul(score_ps[:, b * S:(b + 1) * S], q_rot[:, b].rearrange("p h q -> p (h q)"),
                                                k_rot[:, grp * GROUP + b * S:grp * GROUP + (b + 1) * S],
                                                start=True, stop=True)
                    last.then_inc(scores_done, 1)
                    if s < TICKS - 1:
                        project_queries(s + 1)
                    if s >= 1:
                        pe.wait_ge(o_hi_ready, (tick0 + s) * 2)
                        pe.wait_ge(o_lo_ready, (tick0 + s) * 2)
                        project_output(it * YT, it + 1, s - 1, range(turned_tiles(s)))
                    pe.wait_ge(probs_done, tick0 + (s + 1))
                    pe.wait_ge(probs_copied, tick0 + s)
                    for t in range(GT):
                        last = nc.tensor.transpose(prob_ps[:, t * P:(t + 1) * P], prob_v[:, t * P:(t + 1) * P], eye[:, :])
                    last.then_inc(probs_turned, 1)
                    if s == 0:
                        project_context("V1")
                    else:
                        project_output(it * YT, it + 1, s - 1, range(turned_tiles(s), GT))
                    pe.wait_ge(probs_copied, tick0 + (s + 1))
                    pe.wait_ge(v_copied, it * GROUPS + (1 if s == 0 else 2))
                    pe.wait_ge(o_hi_ready, (tick0 + s) * 2)
                    pe.wait_ge(o_lo_ready, (tick0 + s) * 2)
                    for t in range(GT):
                        for b in range(2):
                            rows = slice(b * S, (b + 1) * S)
                            last = nc.tensor.matmul(attn_ps[b][:, t * P:(t + 1) * P], v_tok[rows, grp * GT + t, :],
                                                    prob_t[rows, t * P:(t + 1) * P], start=True, stop=True)
                    last.then_inc(attn_done, 1)
                    if s == 0:
                        turn_values(1)
                return last_output

            pe.wait_ge(small_landed, 48)
            with pe.Fori(0, HALVES) as half:
                pe.wait_ge(masked_done, half * (KVH * TICKS))
                pe.wait_ge(probs_copied, half * (KVH * TICKS))
                for t in range(TILES):
                    pe.wait_ge(rope_landed[t % 4], half * (16 * TILES // 4) + 16 * (t // 4 + 1))
                    if t == 4:
                        pe.wait_ge(trig_ready, half * TRIG_COPIES + 2)
                    c = (t % 4) * P
                    nc.tensor.transpose(score_ps[:, c:c + P], trig_rows[:, t % 4, 0:D], eye[:, :])
                    nc.tensor.transpose(prob_ps[:, c:c + P], trig_rows[:, t % 4, D:2 * D], eye[:, :]).then_inc(trig_turned, 1)
                pe.wait_ge(trig_ready, half * TRIG_COPIES + TRIG_COPIES)
                iteration(half, half * KVH, True)
                with pe.Fori(1, KVH) as g:
                    last_output = iteration(half, half * KVH + g, False)
                done = (half + 1) * KVH
                last_output(done * YT - YT, done, done * TICKS)
            pe.wait_ge(swap_done, NIT * PROJ)
            pe.wait_ge(cos_done, NIT * ROT)
            with pe.Fori(0, HALVES) as half:
                pe.wait_ge(z_gated, half * TILES)
                turn_tokens(half + HALVES)
                pe.wait_ge(x_hi_ready, (half + HALVES) * TILES + TILES)
                pe.wait_ge(x_lo_ready, (half + HALVES) * TILES + TILES)
                pe.wait_ge(ffn_hi_ready, 3)
                pe.wait_ge(ffn_lo_ready, 3)
                pe.wait_ge(o_lo_ready, NIT * TICKS * 2)
                pe.wait_ge(route_copied, half * GROUPS)
                for j in range(GROUPS):
                    cols = slice(j * GROUP, (j + 1) * GROUP)
                    three_products(attn_ps[j][:, :], [
                        (router_hi[:, c, :], router_lo[:, c, :], x_hi[:, c, cols], x_lo[:, c, cols])
                        for c in range(EC)]).then_inc(route_done, 1)
                pe.wait_ge(route_copied, half * GROUPS + GROUPS)
                pe.wait_ge(logits_copied, half)
                pe.wait_ge(masked_done, NIT * TICKS)
                for t in range(TILES):
                    last = nc.tensor.matmul(score_ps[:, t * EXPERTS:(t + 1) * EXPERTS], route[:, t * P:(t + 1) * P],
                                            keys_sb[:, :], start=True, stop=True)
                last.then_inc(logits_done, 1)

                def bottleneck(t):
                    if t >= 2:
                        pe.wait_ge(z_gated, half * TILES + (t - 1))
                    tok = slice(t * P, (t + 1) * P)
                    three_products(proj_ps[t % 2][:, :], [
                        (x_hi[:, c, tok], x_lo[:, c, tok], a_hi[:, c, :], a_lo[:, c, :])
                        for c in range(EC)]).then_inc(z_done, 1)

                bottleneck(0)
                pe.wait_ge(y_added, NIT * YT)
                pe.wait_ge(probs_copied, NIT * TICKS)
                for t in range(TILES):
                    if t + 1 < TILES:
                        bottleneck(t + 1)
                    pe.wait_ge(z_gated, half * TILES + (t + 1))
                    pe.wait_ge(z_lo_ready, half * TILES + t)
                    for c in range(EC):
                        last = nc.tensor.transpose(prob_ps[:, c * P:(c + 1) * P],
                                                   straight[:, t % 2, c * P:(c + 1) * P], eye[:, :])
                    last.then_inc(z_turned, 1)
                    pe.wait_ge(z_hi_ready, half * TILES + (t + 1))
                    pe.wait_ge(z_lo_ready, half * TILES + (t + 1))
                    pe.wait_ge(final_done, half * TILES + max(t - 1, 0))
                    three_products(y_ps[t % 2][:, :], [
                        (o_hi[:, t % 2, c * P:(c + 1) * P], o_lo[:, t % 2, c * P:(c + 1) * P], b_hi[:, c, :], b_lo[:, c, :])
                        for c in range(EC)]).then_inc(ffn_done, 1)


def kernel(x, ctx_4096, pos_BxS2, mask_BxSxS2_ik0, g_xattn, g_ffn, L0_xattn_Wq, L0_xattn_Wk, L0_xattn_Wv,
           L0_xattn_Wo, L0_ffn_A_w, L0_ffn_B_w, L0_ffn_Wq_w, L0_ffn_keys):
    import numpy as np
    import concourse.bacc as bacc
    from concourse.bass_utils import run_bass_kernel_spmd

    def tiles(a):
        return a.reshape(T // P, P, a.shape[-1]).transpose(1, 0, 2)

    def chunks(a):
        return a.reshape(a.shape[0] // P, P, a.shape[1]).transpose(1, 0, 2)

    def stationary(w, cols):
        return w.reshape(EC, P, w.shape[1] // cols, cols).transpose(2, 1, 0, 3)

    inv_freq = (1.0 / np.float32(10000.0) ** (np.arange(0, D, 2, dtype=np.float32) / np.float32(D))).astype(np.float32)
    angle = np.arange(MAX_POS, dtype=np.float32)[:, None] * inv_freq[None, :]
    cos, sin = np.cos(angle), np.sin(angle)
    rope = np.concatenate([cos, cos, -sin, sin], axis=1).astype(np.float32)

    wk, wv = stationary(L0_xattn_Wk, D), stationary(L0_xattn_Wv, D)
    router = np.zeros((P, EC, P), L0_ffn_Wq_w.dtype)
    router[:, :, 0:ROUTER] = chunks(L0_ffn_Wq_w.T)
    arrays = {
        "x": tiles(x.reshape(T, E)),
        "ctx_t": ctx_4096.reshape(T, E).T,
        "mask": mask_BxSxS2_ik0.transpose(1, 0, 2).reshape(S, B * S),
        "pos": pos_BxS2.reshape(T // P, P).T,
        "gains": np.broadcast_to(np.concatenate([g_xattn, g_ffn]), (P, 2)),
        "wq": stationary(L0_xattn_Wq, 2 * D).reshape(KVH * PAIRS * P, EC * 2 * D),
        "wo": L0_xattn_Wo.reshape(KVH * PAIRS, 2, D, E).transpose(0, 2, 1, 3).reshape(KVH * PAIRS * P, 2 * E),
        "wkv": np.stack([wk, wv], axis=2).reshape(KVH * P, 2 * EC * D),
        "a_t": chunks(L0_ffn_A_w.T),
        "b_t": chunks(L0_ffn_B_w.T),
        "router_t": router,
        "keys_t": L0_ffn_keys.T,
        "rope": rope,
        "ident": np.eye(P, dtype=np.float32),
    }
    nc = bacc.Bacc("TRN2", target_bir_lowering=False, num_devices=1)
    arrays = {f"{n}_dram": np.ascontiguousarray(a) for n, a in arrays.items()}
    args = [nc.dram_tensor(n, a.shape, mybir.dt.from_np(a.dtype), kind="ExternalInput").ap() for n, a in arrays.items()]
    args.append(nc.dram_tensor("out_dram", (P, T // P, E), F32, kind="ExternalOutput").ap())
    flamingo_block(nc, *args)
    result = run_bass_kernel_spmd(nc, [arrays], core_ids=[0]).results[0]["out_dram"]
    return np.ascontiguousarray(result.transpose(1, 0, 2)).reshape(B, S, E)
```

```python
from contextlib import ExitStack

import concourse.bass as bass
from concourse import mybir

F32 = mybir.dt.float32
F32R = mybir.dt.float32r
BF16 = mybir.dt.bfloat16
I32 = mybir.dt.int32
U32 = mybir.dt.uint32
ALU = mybir.AluOpType
ACT = mybir.ActivationFunctionType
AX_X = mybir.AxisListType.X

P = 128
B, S, E = 32, 64, 512
H, KVH, D = 32, 8, 128
T = B * S
HALVES = 2
HT = T // HALVES
TILES = HT // P
HB = B // HALVES
EC = E // P
GROUP = 512
GROUPS = HT // GROUP
GT = GROUP // P
GB = GROUP // S
PAIRS = H // KVH // 2
TICKS = PAIRS * GROUPS
EXPERTS, RANK, TOP_K, ROUTER = 64, 8, 16, 16
N_B = EXPERTS * RANK
FFN_SCALE = 32 / TOP_K
MAX_POS = 512
MASKED = -1.0e30
REMOVED = -3.0e38
EPS = 1e-5
SM_SCALE = 1.0 / float(D) ** 0.5

SEQ = ["K0", "K1", "V0", "Q0a", "Q0b", "Q1a", "Q1b", "V1", "Q2a", "Q2b", "Q3a", "Q3b"]
PROJ = len(SEQ)
ROTATED = [name for name in SEQ if name[0] != "V"]
ROT = len(ROTATED)
YT = TICKS * GT
NIT = HALVES * KVH
POS_STEPS = 4
MOMENT_STEPS = 6
TRIG_COPIES = 2 * GROUPS
X_LOADS = 4
GATE_STEPS = 6
FFN_TILES = HALVES * TILES
FFN_GROUPS = FFN_TILES // GT
LAST = KVH - 1
CONTEXT_READ = SEQ.index("V1") + 1

STATS_AT_EXP = {0: [0], 1: [4]}
STATS_AT_END = {0: [1, 2, 3], 1: [5, 6, 7]}


def projection(name):
    return SEQ.index(name), ROTATED.index(name) if name in ROTATED else None, int(name[1]) % GROUPS


def queries(s):
    return [f"Q{s}a", f"Q{s}b"]


def stage(half, first, closing):
    return half == 0 and first, half == 0 and closing, half == 1 and closing


def turned_tiles(s):
    return GT if s == TICKS - 1 else 2


def flamingo_block(nc, x, ctx_t, mask, pos, gains, wq, wo, wkv, a_t, b_t, router_t, keys_t, rope, ident, out):
    with ExitStack() as stack:
        def sb(name, shape, dt=F32):
            return stack.enter_context(nc.sbuf_tensor(name, shape, dt))

        def bank(name):
            return stack.enter_context(nc.psum_tensor(name, [P, 512], F32))

        def sem(name):
            return stack.enter_context(nc.semaphore(name))

        x_hi = sb("x_hi", [P, EC, HT], F32R)
        x_lo = sb("x_lo", [P, EC, HT], F32R)
        c_hi = sb("c_hi", [P, EC, HT], F32R)
        c_lo = sb("c_lo", [P, EC, HT], F32R)
        resid = sb("resid", [P, HALVES * TILES, E])
        mask_bias = sb("mask_bias", [P, B, S], BF16)
        cos_t = sb("cos_t", [P, HT])
        sin_t = sb("sin_t", [P, HT])
        wq_hi = sb("wq_hi", [P, PAIRS, EC, 2 * D], F32R)
        wq_lo = sb("wq_lo", [P, PAIRS, EC, 2 * D], F32R)
        wo_hi = sb("wo_hi", [P, PAIRS, 2, E], F32R)
        wo_lo = sb("wo_lo", [P, PAIRS, 2, E], F32R)
        wkv_hi = sb("wkv_hi", [P, 2, EC, D], F32R)
        wkv_lo = sb("wkv_lo", [P, 2, EC, D], F32R)
        wq_raw = sb("wq_raw", [P, PAIRS, EC * 2 * D])
        wo_raw = sb("wo_raw", [P, PAIRS, 2 * E])
        wkv_raw = sb("wkv_raw", [P, 2 * EC * D])
        k_rot = sb("k_rot", [P, HT])
        v_tok = sb("v_tok", [P, TILES, D])
        swapped = sb("swapped", [P, 2, GROUP])
        straight = sb("straight", [P, 2, GROUP])
        q_rot = sb("q_rot", [P, GB, 2, S])
        score = sb("score", [P, GB, S])
        expo = sb("expo", [P, GB, S])
        prob = sb("prob", [P, GB, S])
        prob_t = sb("prob_t", [P, 512])
        o_hi = sb("o_hi", [P, 2, GROUP], F32R)
        o_lo = sb("o_lo", [P, 2, GROUP], F32R)
        eye = sb("eye", [P, P])
        row_max = sb("row_max", [P, GB])
        row_sum = sb("row_sum", [P, GB])
        row_inv = sb("row_inv", [P, GB])
        stats = sb("stats", [P, TILES, 6])
        mean = sb("mean", [P, 2, TILES])
        gap = sb("gap", [P, TILES])
        var_eps = sb("var_eps", [P, TILES])
        minus_half = sb("minus_half", [P, TILES])
        rstd = sb("rstd", [P, 2, TILES])
        gain = sb("gain", [P, 2])
        gate_gain = sb("gate_gain", [P, 3])
        pos_i = sb("pos_i", [P, HALVES * TILES], I32)
        pos_f = sb("pos_f", [P, HALVES * TILES])
        pos_w = sb("pos_w", [P, HALVES * TILES])
        pos_u = sb("pos_u", [P, HALVES * TILES], U32)
        keys_sb = sb("keys_sb", [ROUTER, EXPERTS])
        top_a = sb("top_a", [P, GT, 8])
        top_b = sb("top_b", [P, GT, 8])

        proj_ps = [bank("proj_ps0"), bank("proj_ps1")]
        score_ps = bank("score_ps")
        prob_ps = bank("prob_ps")
        attn_ps = [bank("attn_ps0"), bank("attn_ps1")]
        y_ps = [bank("y_ps0"), bank("y_ps1")]

        x_landed = [sem(f"x_landed{i}") for i in range(X_LOADS)]
        x_rest_landed = sem("x_rest_landed")
        ctx_landed = [sem(f"ctx_landed{c}") for c in range(EC)]
        mask_landed = [sem(f"mask_landed{i}") for i in range(HALVES * GROUPS)]
        pos_landed = sem("pos_landed")
        gain_landed = sem("gain_landed")
        small_landed = sem("small_landed")
        wkv_landed = sem("wkv_landed")
        wq_landed = [sem("wq_landed0"), sem("wq_landed1")]
        wo_landed = [sem("wo_landed0"), sem("wo_landed1")]
        rope_landed = [sem(f"rope_landed{i}") for i in range(TILES)]
        a_landed = sem("a_landed")
        b_landed = sem("b_landed")
        router_landed = sem("router_landed")
        out_stored = [sem("out_stored0"), sem("out_stored1")]
        wkv_hi_ready = sem("wkv_hi_ready")
        wkv_lo_ready = sem("wkv_lo_ready")
        wq_hi_ready = [sem("wq_hi_ready0"), sem("wq_hi_ready1")]
        wq_lo_ready = [sem("wq_lo_ready0"), sem("wq_lo_ready1")]
        wo_hi_ready = [sem("wo_hi_ready0"), sem("wo_hi_ready1")]
        wo_lo_ready = [sem("wo_lo_ready0"), sem("wo_lo_ready1")]
        ctx_hi_ready = sem("ctx_hi_ready")
        ctx_lo_ready = sem("ctx_lo_ready")
        ffn_hi_ready = sem("ffn_hi_ready")
        ffn_lo_ready = sem("ffn_lo_ready")
        stats_ready = sem("stats_ready")
        moment_step = sem("moment_step")
        var_ready = sem("var_ready")
        rstd_ready = sem("rstd_ready")
        half_ready = sem("half_ready")
        normed = sem("normed")
        x_turned = sem("x_turned")
        x_hi_ready = sem("x_hi_ready")
        x_lo_ready = sem("x_lo_ready")
        tanh_ready = sem("tanh_ready")
        gain_ready = sem("gain_ready")
        pos_step = sem("pos_step")
        trig_turned = sem("trig_turned")
        trig_ready = sem("trig_ready")
        bias_ready = sem("bias_ready")
        proj_done = sem("proj_done")
        swap_done = sem("swap_done")
        cos_done = sem("cos_done")
        sin_done = sem("sin_done")
        rope_done = sem("rope_done")
        v_turned = sem("v_turned")
        v_copied = sem("v_copied")
        scores_done = sem("scores_done")
        masked_done = sem("masked_done")
        max_done = sem("max_done")
        shift_done = sem("shift_done")
        exp_done = sem("exp_done")
        sum_done = sem("sum_done")
        inv_done = sem("inv_done")
        probs_done = sem("probs_done")
        probs_turned = sem("probs_turned")
        probs_copied = sem("probs_copied")
        even_done = sem("even_done")
        attn_done = sem("attn_done")
        o_hi_ready = sem("o_hi_ready")
        o_lo_ready = sem("o_lo_ready")
        y_done = sem("y_done")
        y_added = sem("y_added")
        route_done = sem("route_done")
        route_copied = sem("route_copied")
        logits_done = sem("logits_done")
        logits_copied = sem("logits_copied")
        topk_step = sem("topk_step")
        gate_exp = sem("gate_exp")
        gate_step = sem("gate_step")
        z_done = sem("z_done")
        z_gated = sem("z_gated")
        z_turned = sem("z_turned")
        z_hi_ready = sem("z_hi_ready")
        z_lo_ready = sem("z_lo_ready")
        ffn_done = sem("ffn_done")
        final_done = sem("final_done")

        prob_v = prob[:, :, :].rearrange("p b k -> p (b k)")
        score_v = score[:, :, :].rearrange("p b k -> p (b k)")
        expo_v = expo[:, :, :].rearrange("p b k -> p (b k)")
        q_rot_v = q_rot[:, :, :, :].rearrange("p (s b) h q -> p s (b h q)", s=2)
        straight_v, swapped_v = [o[:, :, :].rearrange("p s n -> p (s n)") for o in (straight, swapped)]
        normal = [expo_v, prob_v]
        token_ps = [score_ps, prob_ps] + attn_ps * 3
        ctx_raw = [[wq_raw[:, 1, :], wo_raw[:, 0, :], wo_raw[:, 1, :], last] for last in (k_rot[:, :], wq_raw[:, 1, :])]
        mask_raw = [o.bitcast(I32) for o in (q_rot_v[:, 0, :], q_rot_v[:, 1, :], score_v, prob_t[:, :])]

        def rows_in(place):
            return [place.rearrange("p (u w) -> p u w", w=2 * D)[:, t, :] for t in range(GT)]

        trig_rows = [rows_in(straight_v) + rows_in(place)
                     for place in (v_tok[:, :, :].rearrange("p t d -> p (t d)"), swapped_v)]
        trig_ps = [(y_ps[0], y_ps[1]), (proj_ps[0], proj_ps[1])]
        attn_v = [a[:, :].rearrange("p (t h q) -> p t h q", t=GT, h=2) for a in attn_ps]
        o_hi_v = o_hi[:, :, :].rearrange("p h (t b q) -> p b t h q", t=GT, b=2)
        o_lo_v = o_lo[:, :, :].rearrange("p h (t b q) -> p b t h q", t=GT, b=2)
        a_hi, a_lo = c_hi[:, :, 0:N_B], c_lo[:, :, 0:N_B]
        b_hi, b_lo = c_hi[:, :, N_B:N_B + E], c_lo[:, :, N_B:N_B + E]
        a_raw = wq_raw[:, :, :].rearrange("p a (c n) -> p (a c) n", n=N_B)
        b_raw = wo_raw[:, :, :].rearrange("p a (c n) -> p (a c) n", n=E)
        router_raw = wkv_raw[:, 0:EC * P].rearrange("p (c n) -> p c n", c=EC)
        router_hi, router_lo = wkv_hi[:, 0, :, :], wkv_lo[:, 0, :, :]
        route = k_rot[0:ROUTER, 0:GROUP]
        logits, struck, weight = score[:, 0:GT, :], expo[:, 0:GT, :], prob[:, 0:GT, :]
        logits_flat = logits.rearrange("p t e -> p (t e)")
        gate = prob_t[:, :].rearrange("p (k t e) -> p k t e", k=2, t=GT)
        tile_out = q_rot_v

        def tokens_before(k):
            return HALVES * TILES + k * GT

        ffn_splits = [(router_lo, router_raw, router_hi), (a_lo, a_raw, a_hi), (b_lo, b_raw, b_hi)]

        def group_ps(k):
            return proj_ps if k == 0 else attn_ps

        def flat(w):
            return w[:, :, :, :].rearrange("p k c n -> p (k c n)")

        def per_row(ap, n):
            return ap.unsqueeze(2).to_broadcast([P, ap.shape[1], n])

        block = stack.enter_context(nc.Block())

        def tokens_of(half, t):
            return resid[:, half * TILES + t, :]

        def flat3(w):
            return w.rearrange("p c n -> p (c n)")

        @block.sync
        def _(sp):
            def load_context(half, c):
                sp.dma_start(ctx_raw[half][c], ctx_t[c * P:(c + 1) * P, half * HT:(half + 1) * HT]
                             ).then_inc(ctx_landed[c], 16)

            def load_heads(it, g):
                sp.wait_ge(wq_hi_ready[1], it)
                sp.wait_ge(wq_lo_ready[1], it)
                sp.dma_start(wq_raw[:, 1, :], wq[bass.ds((g * PAIRS + 1) * P, P), :]).then_inc(wq_landed[1], 16)
                for pair in range(PAIRS):
                    sp.wait_ge(wo_hi_ready[pair], it)
                    sp.wait_ge(wo_lo_ready[pair], it)
                    sp.dma_start(wo_raw[:, pair, :],
                                 wo[bass.ds((g * PAIRS + pair) * P, P), :]).then_inc(wo_landed[pair], 16)

            def load_next(it, g_next):
                sp.wait_ge(wkv_hi_ready, it + 1)
                sp.wait_ge(wkv_lo_ready, it + 1)
                sp.dma_start(wkv_raw[:, :], wkv[bass.ds(g_next * P, P), :]).then_inc(wkv_landed, 16)
                sp.wait_ge(wq_hi_ready[0], it + 1)
                sp.wait_ge(wq_lo_ready[0], it + 1)
                sp.dma_start(wq_raw[:, 0, :], wq[bass.ds(g_next * (PAIRS * P), P), :]).then_inc(wq_landed[0], 16)

            sp.dma_start(pos_i[:, :], pos).then_inc(pos_landed, 16)
            for c in range(EC):
                load_context(0, c)
            for i in range(X_LOADS):
                few = slice(i * TILES // X_LOADS, (i + 1) * TILES // X_LOADS)
                sp.dma_start(resid[:, few, :], x[:, few, :]).then_inc(x_landed[i], 16)
            sp.dma_start(wq_raw[:, 0, :], wq[0:P, :]).then_inc(wq_landed[0], 16)
            for part, raw in enumerate(mask_raw):
                for r in range(2):
                    sp.dma_start(raw[r * S:(r + 1) * S, :], mask[:, part * GROUP:(part + 1) * GROUP]
                                 ).then_inc(mask_landed[part], 16)
            for half in range(HALVES):
                sp.wait_ge(ctx_hi_ready, (half + 1) * EC)
                sp.wait_ge(ctx_lo_ready, (half + 1) * EC)
                load_heads(half * KVH, 0)
                if half == 0:
                    sp.dma_start(resid[:, TILES:2 * TILES, :], x[:, TILES:2 * TILES, :]).then_inc(x_rest_landed, 16)
                load_next(half * KVH, 1)
                with sp.Fori(1, LAST) as g:
                    load_heads(half * KVH + g, g)
                    load_next(half * KVH + g, g + 1)
                it = half * KVH + LAST
                load_heads(it, LAST)
                if half == 0:
                    load_next(it, 0)
                    for c in range(EC):
                        if c == 0:
                            sp.wait_ge(wq_hi_ready[1], it + 1)
                            sp.wait_ge(wq_lo_ready[1], it + 1)
                        elif c < EC - 1:
                            sp.wait_ge(wo_hi_ready[c - 1], it + 1)
                            sp.wait_ge(wo_lo_ready[c - 1], it + 1)
                        else:
                            sp.wait_ge(ctx_hi_ready, EC + 1)
                            sp.wait_ge(ctx_lo_ready, EC + 1)
                        load_context(1, c)
            sp.wait_ge(wkv_hi_ready, NIT)
            sp.wait_ge(wkv_lo_ready, NIT)
            sp.dma_start(router_raw, router_t).then_inc(router_landed, 16)
            for pair in range(PAIRS):
                sp.wait_ge(wq_hi_ready[pair], NIT)
                sp.wait_ge(wq_lo_ready[pair], NIT)
            sp.dma_start(a_raw, a_t).then_inc(a_landed, 16)
            for pair in range(PAIRS):
                sp.wait_ge(wo_hi_ready[pair], NIT)
                sp.wait_ge(wo_lo_ready[pair], NIT)
            sp.dma_start(b_raw, b_t).then_inc(b_landed, 16)
            for i in range(FFN_TILES):
                sp.wait_ge(final_done, i + 1)
                sp.dma_start(out[:, i, :], tile_out[:, i % 2, :]).then_inc(out_stored[i % 2], 16)
            for s in out_stored:
                sp.wait_ge(s, 16 * (FFN_TILES // 2))

        @block.gpsimd
        def _(pool):
            def weights_lo(lo, raw, hi, hi_ready, lo_ready, n):
                pool.wait_ge(hi_ready, n)
                nc.gpsimd.tensor_tensor(lo, raw, hi.bitcast(F32), ALU.subtract).then_inc(lo_ready, 1)

            def wkv_part(n):
                weights_lo(flat(wkv_lo), wkv_raw[:, :], flat(wkv_hi), wkv_hi_ready, wkv_lo_ready, n)

            def wq_part(pair, n):
                weights_lo(flat3(wq_lo[:, pair]), wq_raw[:, pair, :], flat3(wq_hi[:, pair]),
                           wq_hi_ready[pair], wq_lo_ready[pair], n)

            def wo_part(pair, n):
                weights_lo(flat3(wo_lo[:, pair]), wo_raw[:, pair, :], flat3(wo_hi[:, pair]),
                           wo_hi_ready[pair], wo_lo_ready[pair], n)

            def gather(half):
                for t in range(TILES):
                    pool.wait_ge(rope_done, half * (KVH * ROT))
                    at = half * TILES + t
                    pool.indirect_dma_start(out=trig_rows[half][t], out_offset=None, in_=rope,
                                            in_offset=bass.IndirectOffsetOnAxis(ap=pos_u[:, at:at + 1], axis=0)
                                            ).then_inc(rope_landed[t], 16)

            def context_lo(half, c):
                pool.wait_ge(ctx_hi_ready, half * EC + (c + 1))
                nc.gpsimd.tensor_tensor(c_lo[:, c, :], ctx_raw[half][c], c_hi[:, c, :].bitcast(F32),
                                        ALU.subtract).then_inc(ctx_lo_ready, 1)

            def ffn_lo(n):
                lo, raw, hi = ffn_splits[n]
                pool.wait_ge(ffn_hi_ready, n + 1)
                nc.gpsimd.tensor_tensor(lo, raw, hi.bitcast(F32), ALU.subtract).then_inc(ffn_lo_ready, 1)

            def inverse_root(n):
                pool.wait_ge(var_ready, n + 1)
                nc.gpsimd.tensor_tensor(rstd[:, n % 2, :], var_eps[:, :], minus_half[:, :],
                                        ALU.pow).then_inc(rstd_ready, 1)

            def iteration(half, it, first=False, closing=False):
                start, turnover, ending = stage(half, first, closing)

                def times_sin(name):
                    u, r, grp = projection(name)
                    pool.wait_ge(swap_done, it * PROJ + (u + 1))
                    nc.gpsimd.tensor_tensor(swapped[:, u % 2, :], swapped[:, u % 2, :],
                                            sin_t[:, grp * GROUP:(grp + 1) * GROUP], ALU.mult).then_inc(sin_done, 1)

                if start:
                    inverse_root(0)
                if first:
                    pool.wait_ge(trig_ready, half * TRIG_COPIES + 2)
                times_sin("K0")
                if first:
                    pool.wait_ge(trig_ready, half * TRIG_COPIES + 4)
                times_sin("K1")
                if start:
                    wq_part(0, 1)
                times_sin("Q0a")
                if first:
                    times_sin("Q0b")
                    wq_part(1, it + 1)
                else:
                    wq_part(1, it + 1)
                    times_sin("Q0b")
                wo_part(0, it + 1)
                for s in range(TICKS):
                    if s < TICKS - 1:
                        for name in queries(s + 1):
                            times_sin(name)
                    if s == 0:
                        wo_part(1, it + 1)
                    if s == 1 and turnover:
                        context_lo(1, 0)
                    if s == 1 and ending:
                        ffn_lo(0)
                    if s == 2 and turnover:
                        gather(1)
                        inverse_root(1)
                    if s == 2 and not ending:
                        wkv_part(it + 2)
                    if s == 2 and turnover:
                        context_lo(1, 1)
                        context_lo(1, 2)
                    if s == 2 and ending:
                        ffn_lo(1)
                    if s == 3 and turnover:
                        context_lo(1, 3)
                    if s == 3 and not ending:
                        wq_part(0, it + 2)
                    if s == 3 and ending:
                        inverse_root(HALVES)
                        ffn_lo(2)

            nc.gpsimd.memset(minus_half[:, :], -0.5).then_inc(half_ready, 1)
            pool.wait_ge(half_ready, 1)
            pool.wait_ge(pos_step, POS_STEPS)
            gather(0)
            for half in range(HALVES):
                iteration(half, half * KVH, first=True)
                with pool.Fori(1, LAST) as g:
                    iteration(half, half * KVH + g)
                iteration(half, half * KVH + LAST, closing=True)
            inverse_root(HALVES + 1)

        @block.scalar
        def _(act):
            def weights_hi(hi, raw, landed, ready, n):
                act.wait_ge(landed, 16 * n)
                nc.scalar.copy(hi, raw).then_inc(ready, 1)

            def wkv_part(n):
                weights_hi(flat(wkv_hi), wkv_raw[:, :], wkv_landed, wkv_hi_ready, n)

            def wq_part(pair, n):
                weights_hi(flat3(wq_hi[:, pair]), wq_raw[:, pair, :], wq_landed[pair], wq_hi_ready[pair], n)

            def wo_part(pair, n):
                weights_hi(flat3(wo_hi[:, pair]), wo_raw[:, pair, :], wo_landed[pair], wo_hi_ready[pair], n)

            def turned_hi(half, t):
                act.wait_ge(x_turned, half * TILES + (t + 1))
                nc.scalar.copy(x_hi[:, :, t * P:(t + 1) * P],
                               token_ps[t][:, :].rearrange("p (c n) -> p c n", c=EC)).then_inc(x_hi_ready, 1)

            def context_hi(half, c):
                act.wait_ge(ctx_landed[c], half * 16 + 16)
                if half == 1:
                    act.wait_ge(proj_done, LAST * PROJ + CONTEXT_READ)
                nc.scalar.copy(c_hi[:, c, :], ctx_raw[half][c]).then_inc(ctx_hi_ready, 1)

            def fill_tables(half, grp):
                act.wait_ge(cos_done, half * (ROT * KVH))
                act.wait_ge(sin_done, half * (ROT * KVH))
                act.wait_ge(trig_turned, half * GROUPS + (grp + 1))
                cols = slice(grp * GROUP, (grp + 1) * GROUP)
                for table, ps in zip([cos_t, sin_t], trig_ps[half]):
                    nc.scalar.copy(table[:, cols], ps[:, :]).then_inc(trig_ready, 1)

            def ffn_hi(n):
                _, raw, hi = ffn_splits[n]
                act.wait_ge([router_landed, a_landed, b_landed][n], 16)
                act.wait_ge(proj_done, (NIT - 1) * PROJ + CONTEXT_READ)
                nc.scalar.copy(hi, raw).then_inc(ffn_hi_ready, 1)

            def group_hi(k, t):
                column = (k % 2) * GROUP + t * P
                act.wait_ge(x_turned, tokens_before(k) + t + 1)
                if k == 0:
                    act.wait_ge(proj_done, NIT * PROJ)
                if k >= 2 and t == 0:
                    act.wait_ge(z_done, (k - 1) * GT)
                nc.scalar.copy(x_hi[:, :, column:column + P],
                               group_ps(k)[t % 2][:, :].rearrange("p (c n) -> p c n", c=EC)).then_inc(x_hi_ready, 1)

            def iteration(half, it, first=False, closing=False):
                tick0 = it * TICKS
                start, turnover, ending = stage(half, first, closing)

                def staging_free(u, ahead=0):
                    if u < 2:
                        act.wait_ge(rope_done, (it + ahead) * ROT)
                    else:
                        _, r, _ = projection(SEQ[u - 2])
                        if r is None:
                            act.wait_ge(v_turned, it * GROUPS + (int(SEQ[u - 2][1]) + 1))
                        else:
                            act.wait_ge(rope_done, it * ROT + (r + 1))

                def swap(name, ahead=0):
                    u, r, _ = projection(name)
                    act.wait_ge(proj_done, (it + ahead) * PROJ + (u + 1))
                    staging_free(u, ahead)
                    ps = proj_ps[u % 2]
                    nc.scalar.copy(swapped[0:D // 2, u % 2, :], ps[D // 2:D, :])
                    nc.scalar.copy(swapped[D // 2:D, u % 2, :], ps[0:D // 2, :]).then_inc(swap_done, 1)

                def copy_values(name):
                    u, _, _ = projection(name)
                    act.wait_ge(proj_done, it * PROJ + (u + 1))
                    staging_free(u)
                    nc.scalar.copy(swapped[:, u % 2, :], proj_ps[u % 2][:, :]).then_inc(swap_done, 1)

                if start:
                    fill_tables(0, 0)
                    swap("K0")
                    turned_hi(0, 0)
                    turned_hi(0, 1)
                    fill_tables(0, 1)
                    swap("K1")
                    wq_part(0, 1)
                    copy_values("V0")
                    turned_hi(0, 2)
                    turned_hi(0, 3)
                else:
                    if first:
                        turned_hi(half, 0)
                        turned_hi(half, 1)
                        swap("K0")
                        turned_hi(half, 2)
                        turned_hi(half, 3)
                    swap("K1")
                    copy_values("V0")
                wq_part(1, it + 1)
                swap("Q0a")
                if first:
                    turned_hi(half, 4)
                    turned_hi(half, 5)
                swap("Q0b")
                if first:
                    turned_hi(half, 6)
                    turned_hi(half, 7)
                act.wait_ge(y_done, 0 if start else it * YT - YT // 2)
                wo_part(0, it + 1)
                for s in range(TICKS):
                    act.wait_ge(shift_done, tick0 + (s + 1))
                    act.wait_ge(probs_done, tick0 + s)
                    nc.scalar.activation(expo[:, :, :], score[:, :, :], ACT.Exp, scale=SM_SCALE).then_inc(exp_done, 1)
                    if s < TICKS - 1:
                        for name in queries(s + 1):
                            swap(name)
                    if s == 1 and turnover:
                        context_hi(1, 0)
                    if s == 1 and ending:
                        ffn_hi(0)
                    if s == 2 and not ending:
                        wkv_part(it + 2)
                    if s == 2 and turnover:
                        context_hi(1, 1)
                    if s == 2 and ending:
                        ffn_hi(1)
                    if s == 3 and not ending:
                        wq_part(0, it + 2)
                    if s == 3 and turnover:
                        context_hi(1, 3)
                    if s == 3 and ending:
                        ffn_hi(2)
                    act.wait_ge(probs_turned, tick0 + (s + 1))
                    act.wait_ge(attn_done, tick0 + s)
                    nc.scalar.copy(prob_t[:, :], prob_ps[:, :]).then_inc(probs_copied, 1)
                    if s == 0:
                        copy_values("V1")
                    if s == 3 and turnover:
                        fill_tables(1, 0)
                    if s == 3 and ending:
                        group_hi(0, 0)
                        group_hi(0, 1)
                    if s == TICKS - 1 and not closing:
                        swap("K0", ahead=1)
                    act.wait_ge(y_done, (tick0 + s) * GT)
                    for b, done in enumerate([even_done, attn_done]):
                        act.wait_ge(done, tick0 + (s + 1))
                        nc.scalar.copy(o_hi_v[:, b], attn_v[b]).then_inc(o_hi_ready, 1)
                    if s == 0:
                        wo_part(1, it + 1)
                    if s == 2 and turnover:
                        context_hi(1, 2)
                    if s == 3 and turnover:
                        fill_tables(1, 1)
                    if s == 3 and ending:
                        group_hi(0, 2)
                        group_hi(0, 3)

            act.dma_start(gain[:, :], gains).then_inc(gain_landed, 16)
            act.dma_start(wkv_raw[:, :], wkv[0:P, :]).then_inc(wkv_landed, 16)
            act.dma_start(eye[:, :], ident).then_inc(small_landed, 16)
            act.dma_start(keys_sb[:, :], keys_t).then_inc(small_landed, 16)
            act.wait_ge(gain_landed, 16)
            nc.scalar.activation(gate_gain[:, 0:2], gain[:, :], ACT.Tanh).then_inc(tanh_ready, 1)
            wkv_part(1)
            for c in range(EC):
                context_hi(0, c)
            for half in range(HALVES):
                iteration(half, half * KVH, first=True)
                with act.Fori(1, LAST) as g:
                    iteration(half, half * KVH + g)
                iteration(half, half * KVH + LAST, closing=True)
            def copy_route(k):
                act.wait_ge(route_done, k + 1)
                nc.scalar.copy(route, score_ps[0:ROUTER, :]).then_inc(route_copied, 1)

            def gate_exponential(k):
                act.wait_ge(gate_step, k * GATE_STEPS + 1)
                nc.scalar.activation(weight, weight, ACT.Exp).then_inc(gate_exp, 1)

            copy_route(0)
            group_hi(1, 0)
            group_hi(1, 1)
            gate_exponential(0)
            group_hi(1, 2)
            group_hi(1, 3)
            for i in range(FFN_TILES):
                k, r = divmod(i, GT)
                ahead = k + 1 < FFN_GROUPS
                if r == 0 and ahead and k > 0:
                    group_hi(k + 1, 0)
                    group_hi(k + 1, 1)
                act.wait_ge(z_turned, i + 1)
                if i >= 2:
                    act.wait_ge(ffn_done, i - 1)
                nc.scalar.copy(o_hi[:, i % 2, :], prob_ps[:, :]).then_inc(z_hi_ready, 1)
                if r == 0 and ahead and k > 0:
                    group_hi(k + 1, 2)
                    group_hi(k + 1, 3)
                if r == 1 and ahead:
                    copy_route(k + 1)
                if r == 2 and ahead:
                    gate_exponential(k + 1)

        @block.vector
        def _(dve):
            def row_stats(t, tile):
                nc.vector.bn_stats(stats[:, t, :], tile).then_inc(stats_ready, 1)

            def moments(n):
                mean_a, mean_b = stats[:, :, 1], stats[:, :, 4]
                m, d, v = mean[:, n % 2, :], gap[:, :], var_eps[:, :]
                dve.wait_ge(stats_ready, (n + 1) * TILES)
                nc.vector.tensor_tensor(m, mean_a, mean_b, ALU.add).then_inc(moment_step, 1)
                nc.vector.tensor_tensor(d, mean_a, mean_b, ALU.subtract).then_inc(moment_step, 1)
                dve.wait_ge(rstd_ready, n)
                nc.vector.tensor_tensor(v, stats[:, :, 2], stats[:, :, 5], ALU.add).then_inc(moment_step, 1)
                dve.wait_ge(moment_step, n * MOMENT_STEPS + 3)
                nc.vector.tensor_scalar(m, m, 0.5, None, ALU.mult).then_inc(moment_step, 1)
                nc.vector.tensor_tensor(d, d, d, ALU.mult).then_inc(moment_step, 1)
                nc.vector.tensor_scalar(v, v, 1.0 / E, EPS, ALU.mult, ALU.add).then_inc(moment_step, 1)
                dve.wait_ge(moment_step, n * MOMENT_STEPS + 6)
                nc.vector.scalar_tensor_tensor(out=v, in0=d, scalar=0.25, in1=v,
                                               op0=ALU.mult, op1=ALU.add).then_inc(var_ready, 1)

            def normalise(n, place, at, turned):
                if turned:
                    dve.wait_ge(x_turned, turned)
                t = at % TILES
                nc.vector.tensor_scalar(place, resid[:, at, :], mean[:, n % 2, t:t + 1],
                                        rstd[:, n % 2, t:t + 1], ALU.subtract, ALU.mult).then_inc(normed, 1)

            def token_lo(t, bank_ps, column, before):
                dve.wait_ge(x_hi_ready, before + (t + 1))
                nc.vector.tensor_tensor(x_lo[:, :, column:column + P],
                                        bank_ps[:, :].rearrange("p (c n) -> p c n", c=EC),
                                        x_hi[:, :, column:column + P].bitcast(F32),
                                        ALU.subtract).then_inc(x_lo_ready, 1)

            def make_bias(part):
                dve.wait_ge(mask_landed[part], 32)
                nc.vector.tensor_scalar(mask_bias[:, part * GB:(part + 1) * GB, :].rearrange("p b k -> p (b k)"),
                                        mask_raw[part], 0.0, MASKED, ALU.is_equal, ALU.mult).then_inc(bias_ready, 1)

            def half_stats(half, tiles):
                for t in tiles:
                    row_stats(t, tokens_of(half, t))

            def group_normalise(k, t):
                if t == 0:
                    dve.wait_ge(rstd_ready, HALVES + k * GT // TILES + 1)
                normalise(HALVES + k * GT // TILES, swapped[:, t % 2, :], k * GT + t, tokens_before(k) + t - 1)

            def group_lo(k, t):
                token_lo(t, group_ps(k)[t % 2], (k % 2) * GROUP + t * P, tokens_before(k))

            def iteration(half, it, first=False, closing=False):
                tick0 = it * TICKS
                start, turnover, ending = stage(half, first, closing)

                def times_cos(name):
                    u, r, grp = projection(name)
                    dve.wait_ge(swap_done, it * PROJ + (u + 1))
                    dve.wait_ge(rope_done, it * ROT + max(r - 1, 0))
                    nc.vector.tensor_tensor(straight[:, r % 2, :], proj_ps[u % 2][:, :],
                                            cos_t[:, grp * GROUP:(grp + 1) * GROUP], ALU.mult).then_inc(cos_done, 1)

                def add_rotated(name):
                    u, r, grp = projection(name)
                    dve.wait_ge(cos_done, it * ROT + (r + 1))
                    dve.wait_ge(sin_done, it * ROT + (r + 1))
                    if name[0] == "K":
                        dve.wait_ge(scores_done, tick0)
                        dst = k_rot[:, grp * GROUP:(grp + 1) * GROUP].rearrange("p (b q) -> p b q", q=S)
                    else:
                        dve.wait_ge(scores_done, tick0 + int(name[1]))
                        dst = q_rot[:, :, "ab".index(name[2]), :]
                    nc.vector.tensor_tensor(dst, straight[:, r % 2, :].rearrange("p (b q) -> p b q", q=S),
                                            swapped[:, u % 2, :].rearrange("p (b q) -> p b q", q=S),
                                            ALU.add).then_inc(rope_done, 1)

                def keep_values(j):
                    dve.wait_ge(v_turned, it * GROUPS + (j + 1))
                    dve.wait_ge(attn_done, tick0)
                    nc.vector.tensor_copy(v_tok[:, j * GT:(j + 1) * GT, :].rearrange("p t d -> p (t d)"),
                                          y_ps[j][:, :]).then_inc(v_copied, 1)

                def add_output(s, t):
                    n = it * YT + (s * GT + t) if s >= 0 else it * YT - (GT - t)
                    dve.wait_ge(y_done, n + 1)
                    dve.wait_ge(y_added, n - t)
                    r = tokens_of(0 if s < 0 and first else half, (s % GROUPS) * GT + t)
                    nc.vector.scalar_tensor_tensor(out=r, in0=y_ps[t % 2][:, :], scalar=gate_gain[:, 0:1],
                                                   in1=r, op0=ALU.mult, op1=ALU.add).then_inc(y_added, 1)

                def coming_stats(s, tiles):
                    if s == 0 and turnover:
                        dve.wait_ge(x_rest_landed, 16)
                    if s == 0 and ending:
                        dve.wait_ge(y_added, KVH * YT)
                    dve.wait_ge(var_ready, half + 1)
                    half_stats(1 - half, tiles.get(s, []))

                def first_tiles():
                    dve.wait_ge(rstd_ready, half + 1)
                    dve.wait_ge(probs_turned, tick0)
                    normalise(half, normal[0], half * TILES, 0)
                    normalise(half, normal[1], half * TILES + 1, 0)

                def split_tile(t):
                    if t + 2 < TILES:
                        normalise(half, normal[t % 2], half * TILES + t + 2, half * TILES + t + 1)
                    token_lo(t, token_ps[t], t * P, half * TILES)

                if start:
                    for i in range(X_LOADS):
                        dve.wait_ge(x_landed[i], 16)
                        half_stats(0, range(i * TILES // X_LOADS, (i + 1) * TILES // X_LOADS))
                    moments(0)
                if first:
                    first_tiles()
                if first and not start:
                    split_tile(0)
                    split_tile(1)
                if first:
                    dve.wait_ge(trig_ready, half * TRIG_COPIES + 2)
                times_cos("K0")
                add_rotated("K0")
                if start:
                    split_tile(0)
                    split_tile(1)
                elif first:
                    split_tile(2)
                    split_tile(3)
                if first:
                    dve.wait_ge(trig_ready, half * TRIG_COPIES + 4)
                times_cos("K1")
                add_rotated("K1")
                if start:
                    split_tile(2)
                    split_tile(3)
                keep_values(0)
                if start:
                    for part in range(HALVES * GROUPS):
                        make_bias(part)
                    dve.wait_ge(bias_ready, HALVES * GROUPS)
                times_cos("Q0a")
                if first:
                    split_tile(4)
                add_rotated("Q0a")
                if not start:
                    add_output(-1, 0)
                if first:
                    split_tile(5)
                times_cos("Q0b")
                if not start:
                    add_output(-1, 1)
                add_rotated("Q0b")
                if first:
                    split_tile(6)
                    split_tile(7)
                if not start:
                    add_output(-1, 2)
                    add_output(-1, 3)
                for s in range(TICKS):
                    grp = s % GROUPS
                    seq0 = half * HB + grp * GB
                    bias = mask_bias[:, seq0:seq0 + GB, :].rearrange("p b k -> p (b k)")
                    dve.wait_ge(scores_done, tick0 + (s + 1))
                    dve.wait_ge(exp_done, tick0 + s)
                    nc.vector.tensor_tensor(score_v, score_ps[:, :], bias, ALU.add).then_inc(masked_done, 1)
                    dve.wait_ge(masked_done, tick0 + (s + 1))
                    nc.vector.reduce_max(row_max[:, :], score[:, :, :], AX_X).then_inc(max_done, 1)
                    if s == TICKS - 1:
                        add_output(s - 1, 0)
                    dve.wait_ge(max_done, tick0 + (s + 1))
                    nc.vector.tensor_tensor(score[:, :, :], score[:, :, :], per_row(row_max[:, :], S),
                                            ALU.subtract).then_inc(shift_done, 1)
                    if s == TICKS - 1:
                        add_output(s - 1, 1)
                    if closing:
                        coming_stats(s, STATS_AT_EXP)
                        if s == TICKS - 2:
                            dve.wait_ge(normed, half * TILES)
                            moments(half + 1)
                    dve.wait_ge(exp_done, tick0 + (s + 1))
                    nc.vector.reduce_sum(row_sum[:, :], expo[:, :, :], AX_X).then_inc(sum_done, 1)
                    dve.wait_ge(sum_done, tick0 + (s + 1))
                    nc.vector.reciprocal(row_inv[:, :], row_sum[:, :]).then_inc(inv_done, 1)
                    dve.wait_ge(inv_done, tick0 + (s + 1))
                    dve.wait_ge(probs_turned, tick0 + s)
                    nc.vector.tensor_tensor(prob[:, :, :], expo[:, :, :], per_row(row_inv[:, :], S),
                                            ALU.mult).then_inc(probs_done, 1)
                    if s < TICKS - 1:
                        times_cos(queries(s + 1)[0])
                        add_rotated(queries(s + 1)[0])
                        if s >= 1:
                            add_output(s - 1, 0)
                        times_cos(queries(s + 1)[1])
                        if s >= 1:
                            add_output(s - 1, 1)
                        add_rotated(queries(s + 1)[1])
                        if s >= 1:
                            add_output(s - 1, 2)
                            add_output(s - 1, 3)
                    else:
                        if ending:
                            dve.wait_ge(rope_done, NIT * ROT)
                            group_normalise(0, 0)
                            group_normalise(0, 1)
                        add_output(s - 1, 2)
                        add_output(s - 1, 3)
                        if ending:
                            group_lo(0, 0)
                            group_normalise(0, 2)
                            group_lo(0, 1)
                            group_normalise(0, 3)
                    if closing:
                        coming_stats(s, STATS_AT_END)
                    dve.wait_ge(y_done, (tick0 + s) * GT)
                    for b in range(2):
                        dve.wait_ge(o_hi_ready, (tick0 + s) * 2 + (b + 1))
                        nc.vector.tensor_tensor(o_lo_v[:, b], attn_v[b], o_hi_v[:, b].bitcast(F32),
                                                ALU.subtract).then_inc(o_lo_ready, 1)
                    if s == 0:
                        keep_values(1)
                return add_output

            dve.wait_ge(pos_landed, 16)
            nc.vector.tensor_copy(pos_f[:, :], pos_i[:, :]).then_inc(pos_step, 1)
            dve.wait_ge(pos_step, 1)
            nc.vector.tensor_scalar(pos_w[:, :], pos_f[:, :], 0.0, float(MAX_POS), ALU.is_lt, ALU.mult).then_inc(pos_step, 1)
            dve.wait_ge(pos_step, 2)
            nc.vector.tensor_tensor(pos_f[:, :], pos_f[:, :], pos_w[:, :], ALU.add).then_inc(pos_step, 1)
            dve.wait_ge(pos_step, 3)
            nc.vector.tensor_scalar(pos_u[:, :], pos_f[:, :], 0.0, float(MAX_POS - 1), ALU.max, ALU.min).then_inc(pos_step, 1)
            dve.wait_ge(wkv_hi_ready, 1)
            nc.vector.tensor_tensor(flat(wkv_lo), wkv_raw[:, :], flat(wkv_hi).bitcast(F32),
                                    ALU.subtract).then_inc(wkv_lo_ready, 1)
            for c in range(EC):
                dve.wait_ge(ctx_hi_ready, c + 1)
                nc.vector.tensor_tensor(c_lo[:, c, :], ctx_raw[0][c], c_hi[:, c, :].bitcast(F32),
                                        ALU.subtract).then_inc(ctx_lo_ready, 1)
            dve.wait_ge(tanh_ready, 1)
            nc.vector.tensor_scalar(gate_gain[:, 2:3], gate_gain[:, 1:2], FFN_SCALE, None, ALU.mult).then_inc(gain_ready, 1)
            for half in range(HALVES):
                iteration(half, half * KVH, first=True)
                with dve.Fori(1, LAST) as g:
                    iteration(half, half * KVH + g)
                add_output = iteration(half, half * KVH + LAST, closing=True)
            def gates_top(k):
                n = k * GT
                dve.wait_ge(logits_done, k + 1)
                nc.vector.tensor_copy(logits_flat, score_ps[:, 0:GT * EXPERTS]).then_inc(logits_copied, 1)
                dve.wait_ge(logits_copied, k + 1)
                for t in range(GT):
                    nc.vector.max(top_a[:, t, :], logits[:, t, :]).then_inc(topk_step, 1)
                for t in range(GT):
                    dve.wait_ge(topk_step, n * 4 + t + 1)
                    nc.vector.match_replace(struck[:, t, :], top_a[:, t, :], logits[:, t, :],
                                            REMOVED).then_inc(topk_step, 1)
                for t in range(GT):
                    dve.wait_ge(topk_step, n * 4 + GT + t + 1)
                    nc.vector.max(top_b[:, t, :], struck[:, t, :]).then_inc(topk_step, 1)
                nc.vector.tensor_tensor(weight, logits, top_a[:, 0:GT, 0:1].to_broadcast([P, GT, EXPERTS]),
                                        ALU.subtract).then_inc(gate_step, 1)
                for t in range(GT):
                    dve.wait_ge(topk_step, n * 4 + 2 * GT + t + 1)
                    nc.vector.match_replace(struck[:, t, :], top_b[:, t, :], struck[:, t, :],
                                            REMOVED).then_inc(topk_step, 1)

            def gates_softmax(k):
                dve.wait_ge(topk_step, (k + 1) * GT * 4)
                nc.vector.tensor_tensor(struck, struck, logits, ALU.not_equal).then_inc(gate_step, 1)
                dve.wait_ge(gate_step, k * GATE_STEPS + 2)
                dve.wait_ge(gate_exp, k + 1)
                nc.vector.tensor_tensor(weight, weight, struck, ALU.mult).then_inc(gate_step, 1)
                dve.wait_ge(gate_step, k * GATE_STEPS + 3)
                nc.vector.reduce_sum(row_sum[:, 0:GT], weight, AX_X).then_inc(gate_step, 1)
                dve.wait_ge(gate_step, k * GATE_STEPS + 4)
                nc.vector.reciprocal(row_inv[:, 0:GT], row_sum[:, 0:GT]).then_inc(gate_step, 1)
                dve.wait_ge(gate_step, k * GATE_STEPS + 5)
                nc.vector.tensor_tensor(gate[:, k % 2], weight, per_row(row_inv[:, 0:GT], EXPERTS),
                                        ALU.mult).then_inc(gate_step, 1)
                dve.wait_ge(gate_step, k * GATE_STEPS + 6)

            def gate_bottleneck(i):
                dve.wait_ge(z_done, i + 1)
                if i >= 2:
                    dve.wait_ge(z_turned, i - 1)
                nc.vector.tensor_tensor(straight[:, i % 2, :].rearrange("p (e r) -> p e r", r=RANK),
                                        proj_ps[i % 2][:, :].rearrange("p (e r) -> p e r", r=RANK),
                                        per_row(gate[:, (i // GT) % 2, i % GT, :], RANK), ALU.mult).then_inc(z_gated, 1)

            def bottleneck_lo(i):
                dve.wait_ge(z_hi_ready, i + 1)
                nc.vector.tensor_tensor(o_lo[:, i % 2, :], prob_ps[:, :], o_hi[:, i % 2, :].bitcast(F32),
                                        ALU.subtract).then_inc(z_lo_ready, 1)

            def finish(i):
                dve.wait_ge(ffn_done, i + 1)
                if i >= 2:
                    dve.wait_ge(out_stored[i % 2], 16 * (i // 2))
                nc.vector.scalar_tensor_tensor(out=tile_out[:, i % 2, :], in0=y_ps[i % 2][:, :],
                                               scalar=gate_gain[:, 2:3], in1=resid[:, i, :],
                                               op0=ALU.mult, op1=ALU.add).then_inc(final_done, 1)

            group_lo(0, 2)
            group_lo(0, 3)
            group_normalise(1, 0)
            group_normalise(1, 1)
            add_output(TICKS - 1, 0)
            add_output(TICKS - 1, 1)
            gates_top(0)
            group_lo(1, 0)
            group_normalise(1, 2)
            group_lo(1, 1)
            group_normalise(1, 3)
            add_output(TICKS - 1, 2)
            add_output(TICKS - 1, 3)
            gates_softmax(0)
            gate_bottleneck(0)
            group_lo(1, 2)
            group_lo(1, 3)
            dve.wait_ge(y_added, NIT * YT)
            dve.wait_ge(gain_ready, 1)
            for i in range(FFN_TILES):
                k, r = divmod(i, GT)
                ahead = k + 1 < FFN_GROUPS
                bottleneck_lo(i)
                if r == 3 and k + 2 < FFN_GROUPS:
                    group_normalise(k + 2, 0)
                    group_normalise(k + 2, 1)
                if r == 0 and ahead and k > 0:
                    group_lo(k + 1, 0)
                    group_normalise(k + 1, 2)
                    group_lo(k + 1, 1)
                    group_normalise(k + 1, 3)
                if r == 2 and ahead:
                    gates_top(k + 1)
                if r == 3 and ahead:
                    gates_softmax(k + 1)
                if i + 1 < FFN_TILES:
                    gate_bottleneck(i + 1)
                if r == 0 and ahead and k > 0:
                    group_lo(k + 1, 2)
                    group_lo(k + 1, 3)
                if i == 0:
                    half_stats(1, range(3))
                if i == 1:
                    half_stats(1, range(3, TILES))
                if i == 2:
                    moments(HALVES + 1)
                finish(i)

        @block.tensor
        def _(pe):
            def turn_tile(half, t):
                pe.wait_ge(normed, half * TILES + (t + 1))
                if t == 0:
                    pe.wait_ge(masked_done, half * (KVH * TICKS))
                    pe.wait_ge(probs_copied, half * (KVH * TICKS))
                    pe.wait_ge(o_lo_ready, half * (KVH * TICKS * 2))
                if t >= GT:
                    pe.wait_ge(x_lo_ready, half * TILES + (t - 1))
                for c in range(EC):
                    last = nc.tensor.transpose(token_ps[t][:, c * P:(c + 1) * P],
                                               normal[t % 2][:, c * P:(c + 1) * P], eye[:, :])
                last.then_inc(x_turned, 1)

            def turn_trig(half, grp):
                if grp == 0:
                    pe.wait_ge(cos_done, half * (KVH * ROT))
                else:
                    pe.wait_ge(trig_ready, half * TRIG_COPIES + 2 * grp)
                cos_ps, sin_ps = trig_ps[half]
                for t in range(GT):
                    rows = trig_rows[half][grp * GT + t]
                    pe.wait_ge(rope_landed[grp * GT + t], 16 * (half + 1))
                    cols = slice(t * P, (t + 1) * P)
                    nc.tensor.transpose(cos_ps[:, cols], rows[:, 0:D], eye[:, :])
                    last = nc.tensor.transpose(sin_ps[:, cols], rows[:, D:2 * D], eye[:, :])
                last.then_inc(trig_turned, 1)

            def turn_group(k, t):
                before = tokens_before(k)
                pe.wait_ge(normed, before + t + 1)
                pe.wait_ge(x_lo_ready, before + t - 1)
                for c in range(EC):
                    last = nc.tensor.transpose(group_ps(k)[t % 2][:, c * P:(c + 1) * P],
                                               swapped[:, t % 2, c * P:(c + 1) * P], eye[:, :])
                last.then_inc(x_turned, 1)

            def three_products(ps, parts, begin=True, end=True):
                for i, (l_hi, l_lo, r_hi, r_lo) in enumerate(parts):
                    nc.tensor.matmul(ps, l_hi, r_hi, start=begin and i == 0, stop=False)
                    nc.tensor.matmul(ps, l_hi, r_lo, start=False, stop=False)
                    done = nc.tensor.matmul(ps, l_lo, r_hi, start=False, stop=end and i == len(parts) - 1)
                return done

            def iteration(half, it, first=False, closing=False):
                tick0 = it * TICKS
                start, turnover, ending = stage(half, first, closing)

                def bank_free(u):
                    if u < 2:
                        pe.wait_ge(cos_done, it * ROT)
                        return
                    _, r, _ = projection(SEQ[u - 2])
                    if r is None:
                        pe.wait_ge(swap_done, it * PROJ + (u - 1))
                    else:
                        pe.wait_ge(cos_done, it * ROT + (r + 1))

                def project_context(name, ahead=0):
                    u, _, grp = projection(name)
                    if ahead or name == "K0":
                        pe.wait_ge(cos_done, (it + ahead) * ROT)
                        pe.wait_ge(wkv_hi_ready, it + ahead + 1)
                        pe.wait_ge(wkv_lo_ready, it + ahead + 1)
                    else:
                        bank_free(u)
                    k = "KV".index(name[0])
                    cols = slice(grp * GROUP, (grp + 1) * GROUP)
                    for c in range(EC):
                        if first and name == "K0":
                            pe.wait_ge(ctx_hi_ready, half * EC + (c + 1))
                            pe.wait_ge(ctx_lo_ready, half * EC + (c + 1))
                        done = three_products(proj_ps[u % 2][:, :], [
                            (wkv_hi[:, k, c, :], wkv_lo[:, k, c, :], c_hi[:, c, cols], c_lo[:, c, cols])],
                            begin=c == 0, end=c == EC - 1)
                    done.then_inc(proj_done, 1)

                def project_query(s, head):
                    pair = s // GROUPS
                    u, _, grp = projection(queries(s)[head])
                    pe.wait_ge(wq_hi_ready[pair], it + 1)
                    pe.wait_ge(wq_lo_ready[pair], it + 1)
                    if first:
                        pe.wait_ge(x_hi_ready, half * TILES + (grp + 1) * GT)
                        pe.wait_ge(x_lo_ready, half * TILES + (grp + 1) * GT)
                    cols = slice(grp * GROUP, (grp + 1) * GROUP)
                    bank_free(u)
                    d = slice(head * D, (head + 1) * D)
                    three_products(proj_ps[u % 2][:, :], [
                        (wq_hi[:, pair, c, d], wq_lo[:, pair, c, d], x_hi[:, c, cols], x_lo[:, c, cols])
                        for c in range(EC)]).then_inc(proj_done, 1)

                def turn_values(j):
                    u = SEQ.index(f"V{j}")
                    pe.wait_ge(swap_done, it * PROJ + (u + 1))
                    pe.wait_ge(y_added, it * YT if start or j == 1 else it * YT - GT)
                    for t in range(GT):
                        last = nc.tensor.transpose(y_ps[j][:, t * D:(t + 1) * D],
                                                   swapped[:, u % 2, t * P:(t + 1) * P], eye[:, :])
                    last.then_inc(v_turned, 1)

                def project_output(s, tiles):
                    pair = s % TICKS // GROUPS
                    weights = it + 1 if s >= 0 else it
                    pe.wait_ge(wo_hi_ready[pair], weights)
                    pe.wait_ge(wo_lo_ready[pair], weights)
                    pe.wait_ge(o_hi_ready, (tick0 + (s + 1)) * 2)
                    pe.wait_ge(o_lo_ready, (tick0 + (s + 1)) * 2)
                    for t in tiles:
                        if s == 0 and t < 2:
                            pe.wait_ge(y_added, it * YT)
                            pe.wait_ge(v_copied, it * GROUPS + (t + 1))
                        else:
                            pe.wait_ge(y_added, it * YT + (s * GT + t - 1) if s >= 0 else it * YT - (GT - t + 1))
                        tok = slice(t * P, (t + 1) * P)
                        three_products(y_ps[t % 2][:, :], [
                            (o_hi[:, h, tok], o_lo[:, h, tok], wo_hi[:, pair, h, :], wo_lo[:, pair, h, :])
                            for h in range(2)]).then_inc(y_done, 1)

                if first and not start:
                    turn_tile(half, 0)
                    turn_tile(half, 1)
                    pe.wait_ge(trig_ready, (half + 1) * TRIG_COPIES)
                if first:
                    project_context("K0")
                if first and not start:
                    turn_tile(half, 2)
                    turn_tile(half, 3)
                pe.wait_ge(wkv_hi_ready, it + 1)
                pe.wait_ge(wkv_lo_ready, it + 1)
                project_context("K1")
                if start:
                    turn_trig(0, 0)
                    turn_tile(0, 0)
                    turn_tile(0, 1)
                    turn_trig(0, 1)
                project_context("V0")
                if start:
                    turn_tile(0, 2)
                    turn_tile(0, 3)
                    pe.wait_ge(trig_ready, TRIG_COPIES)
                if first:
                    turn_values(0)
                project_query(0, 0)
                if not first:
                    turn_values(0)
                if first and not start:
                    pe.wait_ge(v_copied, it * GROUPS + 1)
                    project_output(-1, [0])
                if first:
                    turn_tile(half, 4)
                    turn_tile(half, 5)
                project_query(0, 1)
                if not first:
                    pe.wait_ge(v_copied, it * GROUPS + 1)
                    project_output(-1, range(GT))
                if first and not start:
                    project_output(-1, [1])
                if first:
                    turn_tile(half, 6)
                    turn_tile(half, 7)
                if first and not start:
                    project_output(-1, [2, 3])
                for s in range(TICKS):
                    grp = s % GROUPS
                    pe.wait_ge(rope_done, it * ROT + (ROTATED.index(queries(s)[1]) + 1))
                    pe.wait_ge(masked_done, tick0 + s)
                    for b in range(GB):
                        last = nc.tensor.matmul(score_ps[:, b * S:(b + 1) * S], q_rot[:, b].rearrange("p h q -> p (h q)"),
                                                k_rot[:, grp * GROUP + b * S:grp * GROUP + (b + 1) * S],
                                                start=True, stop=True)
                    last.then_inc(scores_done, 1)
                    if s < TICKS - 1:
                        project_query(s + 1, 0)
                        project_query(s + 1, 1)
                    if s >= 1:
                        project_output(s - 1, range(turned_tiles(s)))
                    pe.wait_ge(probs_done, tick0 + (s + 1))
                    pe.wait_ge(probs_copied, tick0 + s)
                    for t in range(GT):
                        last = nc.tensor.transpose(prob_ps[:, t * P:(t + 1) * P], prob_v[:, t * P:(t + 1) * P], eye[:, :])
                    last.then_inc(probs_turned, 1)
                    if s == 0:
                        project_context("V1")
                    else:
                        project_output(s - 1, range(turned_tiles(s), GT))
                    if s == TICKS - 1 and not closing:
                        project_context("K0", ahead=1)
                    if s == TICKS - 1 and turnover:
                        turn_trig(1, 0)
                    if s == TICKS - 1 and ending:
                        pe.wait_ge(cos_done, NIT * ROT)
                        turn_group(0, 0)
                        turn_group(0, 1)
                    pe.wait_ge(probs_copied, tick0 + (s + 1))
                    pe.wait_ge(v_copied, it * GROUPS + (1 if s == 0 else 2))
                    pe.wait_ge(o_hi_ready, (tick0 + s) * 2)
                    pe.wait_ge(o_lo_ready, (tick0 + s) * 2)
                    for b, done in enumerate([even_done, attn_done]):
                        rows = slice(b * S, (b + 1) * S)
                        for t in range(GT):
                            last = nc.tensor.matmul(attn_ps[b][:, t * P:(t + 1) * P], v_tok[rows, grp * GT + t, :],
                                                    prob_t[rows, t * P:(t + 1) * P], start=True, stop=True)
                        last.then_inc(done, 1)
                    if s == 0:
                        turn_values(1)
                    if s == TICKS - 1 and turnover:
                        turn_trig(1, 1)
                    if s == TICKS - 1 and ending:
                        turn_group(0, 2)
                        turn_group(0, 3)
                return project_output

            pe.wait_ge(small_landed, 32)
            for half in range(HALVES):
                iteration(half, half * KVH, first=True)
                with pe.Fori(1, LAST) as g:
                    iteration(half, half * KVH + g)
                project_output = iteration(half, half * KVH + LAST, closing=True)
            def route_group(k):
                pe.wait_ge(x_lo_ready, tokens_before(k + 1))
                if k > 0:
                    pe.wait_ge(logits_copied, k)
                cols = slice((k % 2) * GROUP, (k % 2 + 1) * GROUP)
                three_products(score_ps[:, :], [
                    (router_hi[:, c, :], router_lo[:, c, :], x_hi[:, c, cols], x_lo[:, c, cols])
                    for c in range(EC)]).then_inc(route_done, 1)

            def group_logits(k):
                pe.wait_ge(route_copied, k + 1)
                for t in range(GT):
                    last = nc.tensor.matmul(score_ps[:, t * EXPERTS:(t + 1) * EXPERTS], route[:, t * P:(t + 1) * P],
                                            keys_sb[:, :], start=True, stop=True)
                last.then_inc(logits_done, 1)

            def bottleneck(i):
                if i >= 2:
                    pe.wait_ge(z_gated, i - 1)
                column = (i // GT % 2) * GROUP + (i % GT) * P
                tok = slice(column, column + P)
                three_products(proj_ps[i % 2][:, :], [
                    (x_hi[:, c, tok], x_lo[:, c, tok], a_hi[:, c, :], a_lo[:, c, :])
                    for c in range(EC)]).then_inc(z_done, 1)

            def turn_bottleneck(i):
                pe.wait_ge(z_gated, i + 1)
                pe.wait_ge(z_lo_ready, i)
                for c in range(EC):
                    last = nc.tensor.transpose(prob_ps[:, c * P:(c + 1) * P],
                                               straight[:, i % 2, c * P:(c + 1) * P], eye[:, :])
                last.then_inc(z_turned, 1)

            def expand(i):
                pe.wait_ge(z_hi_ready, i + 1)
                pe.wait_ge(z_lo_ready, i + 1)
                if i >= 2:
                    pe.wait_ge(final_done, i - 1)
                three_products(y_ps[i % 2][:, :], [
                    (o_hi[:, i % 2, c * P:(c + 1) * P], o_lo[:, i % 2, c * P:(c + 1) * P], b_hi[:, c, :], b_lo[:, c, :])
                    for c in range(EC)]).then_inc(ffn_done, 1)

            pe.wait_ge(masked_done, NIT * TICKS)
            pe.wait_ge(ffn_hi_ready, 1)
            pe.wait_ge(ffn_lo_ready, 1)
            project_output(TICKS - 1, [0])
            route_group(0)
            project_output(TICKS - 1, [1])
            group_logits(0)
            turn_group(1, 0)
            turn_group(1, 1)
            project_output(TICKS - 1, [2, 3])
            pe.wait_ge(ffn_hi_ready, 2)
            pe.wait_ge(ffn_lo_ready, 2)
            bottleneck(0)
            turn_group(1, 2)
            turn_group(1, 3)
            bottleneck(1)
            pe.wait_ge(probs_copied, NIT * TICKS)
            pe.wait_ge(o_lo_ready, NIT * TICKS * 2)
            pe.wait_ge(y_added, NIT * YT)
            for i in range(FFN_TILES):
                k, r = divmod(i, GT)
                ahead = k + 1 < FFN_GROUPS
                if r == 0 and ahead and k > 0:
                    turn_group(k + 1, 0)
                    turn_group(k + 1, 1)
                if r == 2 and ahead:
                    group_logits(k + 1)
                turn_bottleneck(i)
                if 0 < i < FFN_TILES - 1:
                    bottleneck(i + 1)
                if r == 0 and ahead and k > 0:
                    turn_group(k + 1, 2)
                    turn_group(k + 1, 3)
                if i == 0 or r == 1 and 0 < k < FFN_GROUPS - 1:
                    route_group(k + 1)
                if i == 0:
                    pe.wait_ge(ffn_hi_ready, 3)
                    pe.wait_ge(ffn_lo_ready, 3)
                expand(i)


def kernel(x, ctx_4096, pos_BxS2, mask_BxSxS2_ik0, g_xattn, g_ffn, L0_xattn_Wq, L0_xattn_Wk, L0_xattn_Wv,
           L0_xattn_Wo, L0_ffn_A_w, L0_ffn_B_w, L0_ffn_Wq_w, L0_ffn_keys):
    import numpy as np
    import concourse.bacc as bacc
    from concourse.bass_utils import run_bass_kernel_spmd

    def tiles(a):
        return a.reshape(T // P, P, a.shape[-1]).transpose(1, 0, 2)

    def chunks(a):
        return a.reshape(a.shape[0] // P, P, a.shape[1]).transpose(1, 0, 2)

    def stationary(w, cols):
        return w.reshape(EC, P, w.shape[1] // cols, cols).transpose(2, 1, 0, 3)

    inv_freq = (1.0 / np.float32(10000.0) ** (np.arange(0, D, 2, dtype=np.float32) / np.float32(D))).astype(np.float32)
    angle = np.arange(MAX_POS, dtype=np.float32)[:, None] * inv_freq[None, :]
    cos, sin = np.cos(angle), np.sin(angle)
    rope = np.concatenate([cos, cos, -sin, sin], axis=1).astype(np.float32)

    wk, wv = stationary(L0_xattn_Wk, D), stationary(L0_xattn_Wv, D)
    router = np.zeros((P, EC, P), L0_ffn_Wq_w.dtype)
    router[:, :, 0:ROUTER] = chunks(L0_ffn_Wq_w.T)
    arrays = {
        "x": tiles(x.reshape(T, E)),
        "ctx_t": ctx_4096.reshape(T, E).T,
        "mask": mask_BxSxS2_ik0.transpose(1, 0, 2).reshape(S, B * S),
        "pos": pos_BxS2.reshape(T // P, P).T,
        "gains": np.broadcast_to(np.concatenate([g_xattn, g_ffn]), (P, 2)),
        "wq": stationary(L0_xattn_Wq, 2 * D).reshape(KVH * PAIRS * P, EC * 2 * D),
        "wo": L0_xattn_Wo.reshape(KVH * PAIRS, 2, D, E).transpose(0, 2, 1, 3).reshape(KVH * PAIRS * P, 2 * E),
        "wkv": np.stack([wk, wv], axis=2).reshape(KVH * P, 2 * EC * D),
        "a_t": chunks(L0_ffn_A_w.T),
        "b_t": chunks(L0_ffn_B_w.T),
        "router_t": router,
        "keys_t": L0_ffn_keys.T,
        "rope": rope,
        "ident": np.eye(P, dtype=np.float32),
    }
    nc = bacc.Bacc("TRN2", target_bir_lowering=False, num_devices=1)
    arrays = {f"{n}_dram": np.ascontiguousarray(a) for n, a in arrays.items()}
    args = [nc.dram_tensor(n, a.shape, mybir.dt.from_np(a.dtype), kind="ExternalInput").ap() for n, a in arrays.items()]
    args.append(nc.dram_tensor("out_dram", (P, T // P, E), F32, kind="ExternalOutput").ap())
    flamingo_block(nc, *args)
    result = run_bass_kernel_spmd(nc, [arrays], core_ids=[0]).results[0]["out_dram"]
    return np.ascontiguousarray(result.transpose(1, 0, 2)).reshape(B, S, E)
```
